# Optimizing a Trainium2 kernel written in Bass

```python
import numpy as np
import jax
import jax.numpy as jnp

def _softmax(x, axis=-1):
    return jax.nn.softmax(x, axis=axis)

def _gelu(x):
    return jax.nn.gelu(x, approximate=True)

def _silu(x):
    return jax.nn.silu(x)

def _sigmoid(x):
    return jax.nn.sigmoid(x)

def _layernorm(x, axis=-1, eps=1e-05):
    m = jnp.mean(x, axis=axis, keepdims=True)
    v = jnp.var(x, axis=axis, keepdims=True)
    return (x - m) / jnp.sqrt(v + eps)

def _scatter_add(tgt, idx, src, axis=0):
    return tgt.at[idx].add(src)

def _segment_sum(src, seg, n):
    return jax.ops.segment_sum(src, seg, n)
kernel_name = 'mk_decoder_preln_d2_seqx_r4_082217'

def setup_inputs(seed: int=0):
    np.random.seed(seed)
    _w = jnp.asarray

    def _rec_inputs():
        import jax
        import jax.numpy as jnp
        _rk = jax.random.key(seed)
        x = 7.22e-05 + 1 * jax.random.normal(jax.random.fold_in(_rk, 1), (2, 1024, 256), jnp.float32)
        _lenS = 1024 - jax.random.randint(jax.random.fold_in(_rk, 7), (2,), 0, max(1, 1024 // 4) + 1, jnp.int32)
        _lenS2 = 77 - jax.random.randint(jax.random.fold_in(_rk, 8), (2,), 0, max(1, 77 // 4) + 1, jnp.int32)
        _ctx_1024P = jax.random.normal(jax.random.fold_in(_rk, 11), (2, 16, 256), jnp.float32)
        _ctx_1024c = jax.random.dirichlet(jax.random.fold_in(_rk, 511), 0.3 * jnp.ones((16,), jnp.float32), (2, 77))
        _ctx_1024t = jnp.einsum('bsk,bkd->bsd', _ctx_1024c, _ctx_1024P)
        _ctx_1024t = _ctx_1024t * jax.lax.rsqrt(jnp.mean(jnp.square(_ctx_1024t)) + 1e-12) * 0.953939
        ctx_1024 = 4.13588e-05 + 0.999923 * (_ctx_1024t + 0.3 * jax.random.normal(jax.random.fold_in(_rk, 611), (2, 77, 256), jnp.float32))
        return (x, ctx_1024)
    x, ctx_1024 = _rec_inputs()

    def _L0_attn_setup():
        import jax, jax.numpy as jnp
        import numpy as np
        D_MODEL = 256
        N_HEADS = 16
        D_HEAD = D_MODEL // N_HEADS
        THRESH = 0.05
        QMAX = 7.0

        def _ternary_weight(W):
            a = jnp.abs(W)
            delta = THRESH * jnp.mean(a)
            mask = (a > delta).astype(W.dtype)
            tern = jnp.sign(W) * mask
            alpha = jnp.sum(a * mask) / jnp.maximum(jnp.sum(mask), 1.0)
            q = alpha * tern
            return W + jax.lax.stop_gradient(q - W)

        def _fp4_act(y):
            scale = jnp.maximum(jnp.max(jnp.abs(y)) / QMAX, 1e-08)
            q = jnp.clip(jnp.round(y / scale), -QMAX, QMAX) * scale
            return y + jax.lax.stop_gradient(q - y)
        key = jax.random.key(seed)
        ks = jax.random.split(key, 5)
        std = 1.0 / np.sqrt(D_MODEL)
        x = jax.random.normal(ks[0], (2, 512, D_MODEL), dtype=jnp.float32)
        Wq = jax.random.normal(ks[1], (D_MODEL, D_MODEL), dtype=jnp.float32) * std
        Wk = jax.random.normal(ks[2], (D_MODEL, D_MODEL), dtype=jnp.float32) * std
        Wv = jax.random.normal(ks[3], (D_MODEL, D_MODEL), dtype=jnp.float32) * std
        Wo = jax.random.normal(ks[4], (D_MODEL, D_MODEL), dtype=jnp.float32) * std
        z = jnp.zeros((D_MODEL,), dtype=jnp.float32)
        return {'x': x, 'Wq': Wq, 'bq': z, 'Wk': Wk, 'bk': z, 'Wv': Wv, 'bv': z, 'Wo': Wo, 'bo': z}
    _L0_attn_all = _L0_attn_setup()
    _L0_attn_in = {k: v for k, v in _L0_attn_all.items() if k in ('Wq', 'bq', 'Wk', 'bk', 'Wv', 'bv', 'Wo', 'bo')}
    del _L0_attn_all

    def _L0_xattn_setup():
        import jax, jax.numpy as jnp
        import numpy as np
        D_MODEL = 256
        NUM_HEADS = 16
        DEPTH = D_MODEL // NUM_HEADS

        def _split_heads(x, B):
            return x.reshape(B, -1, NUM_HEADS, DEPTH).transpose(0, 2, 1, 3)
        key = jax.random.key(seed)
        ks = jax.random.split(key, 10)
        B, LQ, LK = (4, 512, 512)
        bound = float(np.sqrt(6.0 / (D_MODEL + D_MODEL)))

        def w(k):
            return jax.random.uniform(k, (D_MODEL, D_MODEL), jnp.float32, -bound, bound)
        return {'query': jax.random.normal(ks[0], (B, LQ, D_MODEL), jnp.float32), 'value': jax.random.normal(ks[1], (B, LK, D_MODEL), jnp.float32), 'wq': w(ks[2]), 'bq': jnp.zeros((D_MODEL,), jnp.float32), 'wk': w(ks[3]), 'bk': jnp.zeros((D_MODEL,), jnp.float32), 'wv': w(ks[4]), 'bv': jnp.zeros((D_MODEL,), jnp.float32), 'wo': w(ks[5]), 'bo': jnp.zeros((D_MODEL,), jnp.float32)}
    _L0_xattn_all = _L0_xattn_setup()
    _L0_xattn_in = {k: v for k, v in _L0_xattn_all.items() if k in ('wq', 'bq', 'wk', 'bk', 'wv', 'bv', 'wo', 'bo')}
    del _L0_xattn_all

    def _L0_ffn_setup():
        import jax, jax.numpy as jnp
        import numpy as np
        key = jax.random.key(seed)
        ks = jax.random.split(key, 5)
        B, Sq, M, E, H = (4, 512, 256, 8, 1024)
        x = jax.random.normal(ks[0], (B, Sq, M), dtype=jnp.float32)
        wg = jax.random.normal(ks[1], (M, E), dtype=jnp.float32) * (1.0 / np.sqrt(M))
        w1 = jax.random.normal(ks[2], (E, M, H), dtype=jnp.float32) * (1.0 / np.sqrt(M))
        b1 = jnp.zeros((E, H), dtype=jnp.float32)
        w2 = jax.random.normal(ks[3], (E, H, M), dtype=jnp.float32) * (1.0 / np.sqrt(H))
        b2 = jnp.zeros((E, M), dtype=jnp.float32)
        return {'x': x, 'wg': wg, 'w1': w1, 'b1': b1, 'w2': w2, 'b2': b2}
    _L0_ffn_all = _L0_ffn_setup()
    _L0_ffn_in = {k: v for k, v in _L0_ffn_all.items() if k in ('wg', 'w1', 'b1', 'w2', 'b2')}
    del _L0_ffn_all

    def _L1_attn_setup():
        import jax, jax.numpy as jnp
        import numpy as np
        D_MODEL = 256
        NUM_HEADS = 16
        D_K = D_MODEL // NUM_HEADS
        ROPE_BASE = 10000.0

        def _rope_cos_sin(seq_len, d_k):
            inv_freq = 1.0 / ROPE_BASE ** (jnp.arange(0, d_k, 2, dtype=jnp.float32) / d_k)
            t = jnp.arange(seq_len, dtype=jnp.float32)
            freqs = t[:, None] * inv_freq[None, :]
            emb = jnp.concatenate([freqs, freqs], axis=-1)
            return (jnp.cos(emb)[None, None], jnp.sin(emb)[None, None])

        def _apply_rope(q, k, cos, sin):
            q1, q2 = (q[..., ::2], q[..., 1::2])
            k1, k2 = (k[..., ::2], k[..., 1::2])
            q_rot = jnp.concatenate([-q2, q1], axis=-1)
            k_rot = jnp.concatenate([-k2, k1], axis=-1)
            return (q * cos + q_rot * sin, k * cos + k_rot * sin)
        key = jax.random.key(seed)
        ks = jax.random.split(key, 5)
        B, S = (2, 512)
        x = jax.random.normal(ks[0], (B, S, D_MODEL), dtype=jnp.float32)
        scale = 1.0 / np.sqrt(D_MODEL)
        Wq = jax.random.normal(ks[1], (D_MODEL, D_MODEL), dtype=jnp.float32) * scale
        Wk = jax.random.normal(ks[2], (D_MODEL, D_MODEL), dtype=jnp.float32) * scale
        Wv = jax.random.normal(ks[3], (D_MODEL, D_MODEL), dtype=jnp.float32) * scale
        Wo = jax.random.normal(ks[4], (D_MODEL, D_MODEL), dtype=jnp.float32) * scale
        return {'x': x, 'Wq': Wq, 'Wk': Wk, 'Wv': Wv, 'Wo': Wo}
    _L1_attn_all = _L1_attn_setup()
    _L1_attn_in = {k: v for k, v in _L1_attn_all.items() if k in ('Wq', 'Wk', 'Wv', 'Wo')}
    del _L1_attn_all

    def _L1_xattn_setup():
        import jax, jax.numpy as jnp
        import numpy as np
        D_MODEL = 256
        N_HEADS = 16
        D_HEAD = D_MODEL // N_HEADS
        key = jax.random.key(seed)
        ks = jax.random.split(key, 11)
        B, T = (2, 512)
        s = 1.0 / np.sqrt(D_MODEL)
        return {'query': jax.random.normal(ks[0], (B, T, D_MODEL), dtype=jnp.float32), 'key': jax.random.normal(ks[1], (B, T, D_MODEL), dtype=jnp.float32), 'value': jax.random.normal(ks[2], (B, T, D_MODEL), dtype=jnp.float32), 'Wq': jax.random.normal(ks[3], (D_MODEL, D_MODEL), dtype=jnp.float32) * s, 'bq': jnp.zeros((D_MODEL,), dtype=jnp.float32), 'Wk': jax.random.normal(ks[4], (D_MODEL, D_MODEL), dtype=jnp.float32) * s, 'bk': jnp.zeros((D_MODEL,), dtype=jnp.float32), 'Wv': jax.random.normal(ks[5], (D_MODEL, D_MODEL), dtype=jnp.float32) * s, 'bv': jnp.zeros((D_MODEL,), dtype=jnp.float32), 'Wh': jax.random.normal(ks[6], (D_MODEL, D_MODEL), dtype=jnp.float32) * s, 'bh': jnp.zeros((D_MODEL,), dtype=jnp.float32)}
    _L1_xattn_all = _L1_xattn_setup()
    _L1_xattn_in = {k: v for k, v in _L1_xattn_all.items() if k in ('Wq', 'bq', 'Wk', 'bk', 'Wv', 'bv', 'Wh', 'bh')}
    del _L1_xattn_all

    def _L1_ffn_setup():
        import jax, jax.numpy as jnp
        import numpy as np
        LATENT = 256
        LEAF_W = 64
        DEPTH = 4
        N_LEAVES = 2 ** DEPTH
        N_NODES = 2 ** DEPTH - 1
        B, S = (4, 512)

        def _fff_params(key, prefix):
            ks = jax.random.split(key, 4)
            d, h, l, n = (LATENT, LEAF_W, N_LEAVES, N_NODES)
            s_in = 1.0 / np.sqrt(d).astype(np.float32)
            s_h = 1.0 / np.sqrt(h).astype(np.float32)
            return {f'{prefix}_node_w': jax.random.normal(ks[0], (n, d), jnp.float32) * s_in, f'{prefix}_node_b': jax.random.normal(ks[1], (n,), jnp.float32) * s_in, f'{prefix}_w1': jax.random.normal(ks[2], (l, d, h), jnp.float32) * s_in, f'{prefix}_b1': jnp.zeros((l, h), jnp.float32), f'{prefix}_w2': jax.random.normal(ks[3], (l, h, d), jnp.float32) * s_h, f'{prefix}_b2': jnp.zeros((l, d), jnp.float32)}

        def _fff(x, node_w, node_b, w1, b1, w2, b2):
            Bx, Sx, D = x.shape
            xf = x.reshape(-1, D)
            N = xf.shape[0]
            cur = jnp.zeros((N,), jnp.int32)
            for _ in range(DEPTH):
                pw = node_w[cur]
                score = jnp.einsum('nd,nd->n', xf, pw) + node_b[cur]
                cur = 2 * cur + 1 + (score >= 0).astype(jnp.int32)
            leaf = cur - N_NODES
            sel = jax.nn.one_hot(leaf, N_LEAVES, dtype=xf.dtype)
            hidden_all = jax.nn.relu(jnp.einsum('nd,ldh->lnh', xf, w1) + b1[:, None, :])
            hidden = hidden_all * sel.T[:, :, None]
            out = jnp.einsum('lnh,lho->no', hidden, w2) + sel @ b2
            return out.reshape(Bx, Sx, D)
        key = jax.random.key(seed)
        kx, kq, kk, kv = jax.random.split(key, 4)
        inp = {'x': jax.random.normal(kx, (B, S, LATENT), jnp.float32)}
        inp.update(_fff_params(kq, 'q'))
        inp.update(_fff_params(kk, 'k'))
        inp.update(_fff_params(kv, 'v'))
        return inp
    _L1_ffn_all = _L1_ffn_setup()
    _L1_ffn_in = {k: v for k, v in _L1_ffn_all.items() if k in ('q_node_w', 'q_node_b', 'q_w1', 'q_b1', 'q_w2', 'q_b2', 'k_node_w', 'k_node_b', 'k_w1', 'k_b1', 'k_w2', 'k_b2', 'v_node_w', 'v_node_b', 'v_w1', 'v_b1', 'v_w2', 'v_b2')}
    del _L1_ffn_all
    return {'x': x, 'ctx_1024': ctx_1024, 'L0_attn_Wq': _L0_attn_in['Wq'], 'L0_attn_bq': _L0_attn_in['bq'], 'L0_attn_Wk': _L0_attn_in['Wk'], 'L0_attn_bk': _L0_attn_in['bk'], 'L0_attn_Wv': _L0_attn_in['Wv'], 'L0_attn_bv': _L0_attn_in['bv'], 'L0_attn_Wo': _L0_attn_in['Wo'], 'L0_attn_bo': _L0_attn_in['bo'], 'L0_xattn_wq': _L0_xattn_in['wq'], 'L0_xattn_bq': _L0_xattn_in['bq'], 'L0_xattn_wk': _L0_xattn_in['wk'], 'L0_xattn_bk': _L0_xattn_in['bk'], 'L0_xattn_wv': _L0_xattn_in['wv'], 'L0_xattn_bv': _L0_xattn_in['bv'], 'L0_xattn_wo': _L0_xattn_in['wo'], 'L0_xattn_bo': _L0_xattn_in['bo'], 'L0_ffn_wg': _L0_ffn_in['wg'], 'L0_ffn_w1': _L0_ffn_in['w1'], 'L0_ffn_b1': _L0_ffn_in['b1'], 'L0_ffn_w2': _L0_ffn_in['w2'], 'L0_ffn_b2': _L0_ffn_in['b2'], 'L1_attn_Wq': _L1_attn_in['Wq'], 'L1_attn_Wk': _L1_attn_in['Wk'], 'L1_attn_Wv': _L1_attn_in['Wv'], 'L1_attn_Wo': _L1_attn_in['Wo'], 'L1_xattn_Wq': _L1_xattn_in['Wq'], 'L1_xattn_bq': _L1_xattn_in['bq'], 'L1_xattn_Wk': _L1_xattn_in['Wk'], 'L1_xattn_bk': _L1_xattn_in['bk'], 'L1_xattn_Wv': _L1_xattn_in['Wv'], 'L1_xattn_bv': _L1_xattn_in['bv'], 'L1_xattn_Wh': _L1_xattn_in['Wh'], 'L1_xattn_bh': _L1_xattn_in['bh'], 'L1_ffn_q_node_w': _L1_ffn_in['q_node_w'], 'L1_ffn_q_node_b': _L1_ffn_in['q_node_b'], 'L1_ffn_q_w1': _L1_ffn_in['q_w1'], 'L1_ffn_q_b1': _L1_ffn_in['q_b1'], 'L1_ffn_q_w2': _L1_ffn_in['q_w2'], 'L1_ffn_q_b2': _L1_ffn_in['q_b2'], 'L1_ffn_k_node_w': _L1_ffn_in['k_node_w'], 'L1_ffn_k_node_b': _L1_ffn_in['k_node_b'], 'L1_ffn_k_w1': _L1_ffn_in['k_w1'], 'L1_ffn_k_b1': _L1_ffn_in['k_b1'], 'L1_ffn_k_w2': _L1_ffn_in['k_w2'], 'L1_ffn_k_b2': _L1_ffn_in['k_b2'], 'L1_ffn_v_node_w': _L1_ffn_in['v_node_w'], 'L1_ffn_v_node_b': _L1_ffn_in['v_node_b'], 'L1_ffn_v_w1': _L1_ffn_in['v_w1'], 'L1_ffn_v_b1': _L1_ffn_in['v_b1'], 'L1_ffn_v_w2': _L1_ffn_in['v_w2'], 'L1_ffn_v_b2': _L1_ffn_in['v_b2']}

def reference(x, ctx_1024, L0_attn_Wq, L0_attn_bq, L0_attn_Wk, L0_attn_bk, L0_attn_Wv, L0_attn_bv, L0_attn_Wo, L0_attn_bo, L0_xattn_wq, L0_xattn_bq, L0_xattn_wk, L0_xattn_bk, L0_xattn_wv, L0_xattn_bv, L0_xattn_wo, L0_xattn_bo, L0_ffn_wg, L0_ffn_w1, L0_ffn_b1, L0_ffn_w2, L0_ffn_b2, L1_attn_Wq, L1_attn_Wk, L1_attn_Wv, L1_attn_Wo, L1_xattn_Wq, L1_xattn_bq, L1_xattn_Wk, L1_xattn_bk, L1_xattn_Wv, L1_xattn_bv, L1_xattn_Wh, L1_xattn_bh, L1_ffn_q_node_w, L1_ffn_q_node_b, L1_ffn_q_w1, L1_ffn_q_b1, L1_ffn_q_w2, L1_ffn_q_b2, L1_ffn_k_node_w, L1_ffn_k_node_b, L1_ffn_k_w1, L1_ffn_k_b1, L1_ffn_k_w2, L1_ffn_k_b2, L1_ffn_v_node_w, L1_ffn_v_node_b, L1_ffn_v_w1, L1_ffn_v_b1, L1_ffn_v_w2, L1_ffn_v_b2):
    import jax
    import jax.numpy as jnp

    def _L0_attn_ref(x, Wq, bq, Wk, bk, Wv, bv, Wo, bo):
        import jax, jax.numpy as jnp
        import numpy as np
        D_MODEL = 256
        N_HEADS = 16
        D_HEAD = D_MODEL // N_HEADS
        THRESH = 0.05
        QMAX = 7.0

        def _ternary_weight(W):
            a = jnp.abs(W)
            delta = THRESH * jnp.mean(a)
            mask = (a > delta).astype(W.dtype)
            tern = jnp.sign(W) * mask
            alpha = jnp.sum(a * mask) / jnp.maximum(jnp.sum(mask), 1.0)
            q = alpha * tern
            return W + jax.lax.stop_gradient(q - W)

        def _fp4_act(y):
            scale = jnp.maximum(jnp.max(jnp.abs(y)) / QMAX, 1e-08)
            q = jnp.clip(jnp.round(y / scale), -QMAX, QMAX) * scale
            return y + jax.lax.stop_gradient(q - y)
        B, T, C = x.shape
        H, Dh = (N_HEADS, D_HEAD)

        def proj(W, b):
            y = jnp.einsum('btc,oc->bto', x, _ternary_weight(W)) + b
            return y.reshape(B, T, H, Dh).transpose(0, 2, 1, 3)
        q = proj(Wq, bq)
        k = proj(Wk, bk)
        v = proj(Wv, bv)
        att = jnp.einsum('bhtd,bhsd->bhts', q, k) / jnp.sqrt(jnp.asarray(Dh, x.dtype))
        att = jax.nn.softmax(att, axis=-1)
        y = jnp.einsum('bhts,bhsd->bhtd', att, v)
        y = y.transpose(0, 2, 1, 3).reshape(B, T, C)
        y = jnp.einsum('btc,oc->bto', y, _ternary_weight(Wo)) + bo
        return _fp4_act(y)

    def _L0_xattn_ref(query, value, wq, bq, wk, bk, wv, bv, wo, bo):
        import jax, jax.numpy as jnp
        import numpy as np
        D_MODEL = 256
        NUM_HEADS = 16
        DEPTH = D_MODEL // NUM_HEADS

        def _split_heads(x, B):
            return x.reshape(B, -1, NUM_HEADS, DEPTH).transpose(0, 2, 1, 3)
        B = query.shape[0]
        q = _split_heads(query @ wq.T + bq, B)
        k = _split_heads(value @ wk.T + bk, B)
        v = _split_heads(value @ wv.T + bv, B)
        scale = jnp.sqrt(jnp.asarray(DEPTH, dtype=q.dtype))
        scores = jnp.einsum('bhqd,bhkd->bhqk', q, k) / scale
        attn = jax.nn.softmax(scores, axis=-1)
        ctx = jnp.einsum('bhqk,bhkd->bhqd', attn, v)
        ctx = ctx.transpose(0, 2, 1, 3).reshape(B, -1, D_MODEL)
        return ctx @ wo.T + bo

    def _L0_ffn_ref(x, wg, w1, b1, w2, b2):
        import jax, jax.numpy as jnp
        import numpy as np
        B, Sq, M = x.shape
        E = wg.shape[1]
        S = B * Sq
        C = S // E
        xt = x.reshape(S, M)
        gates = jax.nn.softmax(xt @ wg, axis=-1)
        expert_idx = jnp.argmax(gates, axis=-1)
        mask1 = jax.nn.one_hot(expert_idx, E, dtype=xt.dtype)
        locations = jnp.cumsum(mask1, axis=0) - 1.0
        pos = jnp.sum(locations * mask1, axis=1).astype(jnp.int32)
        keep = (pos < C).astype(xt.dtype)
        gate_val = jnp.sum(gates * mask1, axis=1) * keep
        slot = expert_idx.astype(jnp.int32) * C + jnp.clip(pos, 0, C - 1)
        disp = jnp.zeros((E * C, M), dtype=xt.dtype).at[slot].add(xt * keep[:, None])
        disp = disp.reshape(E, C, M)
        h = jax.nn.relu(jnp.einsum('ecm,emh->ech', disp, w1) + b1[:, None, :])
        eo = jnp.einsum('ech,ehm->ecm', h, w2) + b2[:, None, :]
        out = eo.reshape(E * C, M)[slot] * gate_val[:, None]
        return out.reshape(B, Sq, M)

    def _L1_attn_ref(x, Wq, Wk, Wv, Wo):
        import jax, jax.numpy as jnp
        import numpy as np
        D_MODEL = 256
        NUM_HEADS = 16
        D_K = D_MODEL // NUM_HEADS
        ROPE_BASE = 10000.0

        def _rope_cos_sin(seq_len, d_k):
            inv_freq = 1.0 / ROPE_BASE ** (jnp.arange(0, d_k, 2, dtype=jnp.float32) / d_k)
            t = jnp.arange(seq_len, dtype=jnp.float32)
            freqs = t[:, None] * inv_freq[None, :]
            emb = jnp.concatenate([freqs, freqs], axis=-1)
            return (jnp.cos(emb)[None, None], jnp.sin(emb)[None, None])

        def _apply_rope(q, k, cos, sin):
            q1, q2 = (q[..., ::2], q[..., 1::2])
            k1, k2 = (k[..., ::2], k[..., 1::2])
            q_rot = jnp.concatenate([-q2, q1], axis=-1)
            k_rot = jnp.concatenate([-k2, k1], axis=-1)
            return (q * cos + q_rot * sin, k * cos + k_rot * sin)
        B, S, D = x.shape
        H, dk = (NUM_HEADS, D_K)

        def proj(W):
            return (x @ W.T).reshape(B, S, H, dk).transpose(0, 2, 1, 3)
        q, k, v = (proj(Wq), proj(Wk), proj(Wv))
        cos, sin = _rope_cos_sin(S, dk)
        q, k = _apply_rope(q, k, cos, sin)
        scores = jnp.einsum('bhqd,bhkd->bhqk', q, k) / jnp.sqrt(jnp.float32(dk))
        attn = jax.nn.softmax(scores, axis=-1)
        out = jnp.einsum('bhqk,bhkd->bhqd', attn, v)
        out = out.transpose(0, 2, 1, 3).reshape(B, S, D)
        return out @ Wo.T

    def _L1_xattn_ref(query, key, value, Wq, bq, Wk, bk, Wv, bv, Wh, bh):
        import jax, jax.numpy as jnp
        import numpy as np
        D_MODEL = 256
        N_HEADS = 16
        D_HEAD = D_MODEL // N_HEADS
        B, T_src, _ = query.shape
        T_dst = key.shape[1]
        Q = query @ Wq.T + bq
        K = key @ Wk.T + bk
        V = value @ Wv.T + bv
        Q = Q.reshape(B, T_src, N_HEADS, D_HEAD).transpose(0, 2, 1, 3)
        K = K.reshape(B, T_dst, N_HEADS, D_HEAD).transpose(0, 2, 1, 3)
        V = V.reshape(B, T_dst, N_HEADS, D_HEAD).transpose(0, 2, 1, 3)
        dot = jnp.einsum('bhsd,bhtd->bhst', Q, K) / np.sqrt(D_HEAD)
        scores = jax.nn.softmax(dot, axis=-1)
        out = jnp.einsum('bhst,bhtd->bhsd', scores, V)
        out = out.reshape(B, T_src, D_MODEL)
        return out @ Wh.T + bh

    def _L1_ffn_ref(x, q_node_w, q_node_b, q_w1, q_b1, q_w2, q_b2, k_node_w, k_node_b, k_w1, k_b1, k_w2, k_b2, v_node_w, v_node_b, v_w1, v_b1, v_w2, v_b2):
        import jax, jax.numpy as jnp
        import numpy as np
        LATENT = 256
        LEAF_W = 64
        DEPTH = 4
        N_LEAVES = 2 ** DEPTH
        N_NODES = 2 ** DEPTH - 1
        B, S = (4, 512)

        def _fff_params(key, prefix):
            ks = jax.random.split(key, 4)
            d, h, l, n = (LATENT, LEAF_W, N_LEAVES, N_NODES)
            s_in = 1.0 / np.sqrt(d).astype(np.float32)
            s_h = 1.0 / np.sqrt(h).astype(np.float32)
            return {f'{prefix}_node_w': jax.random.normal(ks[0], (n, d), jnp.float32) * s_in, f'{prefix}_node_b': jax.random.normal(ks[1], (n,), jnp.float32) * s_in, f'{prefix}_w1': jax.random.normal(ks[2], (l, d, h), jnp.float32) * s_in, f'{prefix}_b1': jnp.zeros((l, h), jnp.float32), f'{prefix}_w2': jax.random.normal(ks[3], (l, h, d), jnp.float32) * s_h, f'{prefix}_b2': jnp.zeros((l, d), jnp.float32)}

        def _fff(x, node_w, node_b, w1, b1, w2, b2):
            Bx, Sx, D = x.shape
            xf = x.reshape(-1, D)
            N = xf.shape[0]
            cur = jnp.zeros((N,), jnp.int32)
            for _ in range(DEPTH):
                pw = node_w[cur]
                score = jnp.einsum('nd,nd->n', xf, pw) + node_b[cur]
                cur = 2 * cur + 1 + (score >= 0).astype(jnp.int32)
            leaf = cur - N_NODES
            sel = jax.nn.one_hot(leaf, N_LEAVES, dtype=xf.dtype)
            hidden_all = jax.nn.relu(jnp.einsum('nd,ldh->lnh', xf, w1) + b1[:, None, :])
            hidden = hidden_all * sel.T[:, :, None]
            out = jnp.einsum('lnh,lho->no', hidden, w2) + sel @ b2
            return out.reshape(Bx, Sx, D)
        q = _fff(x, q_node_w, q_node_b, q_w1, q_b1, q_w2, q_b2)
        k = _fff(x, k_node_w, k_node_b, k_w1, k_b1, k_w2, k_b2)
        v = _fff(x, v_node_w, v_node_b, v_w1, v_b1, v_w2, v_b2)
        scale = 1.0 / np.sqrt(LATENT).astype(np.float32)
        attn = jax.nn.softmax(jnp.einsum('bqd,bkd->bqk', q, k) * scale, axis=-1)
        return jnp.einsum('bqk,bkd->bqd', attn, v)
    x = x + _L0_attn_ref(_layernorm(x, axis=-1), L0_attn_Wq, L0_attn_bq, L0_attn_Wk, L0_attn_bk, L0_attn_Wv, L0_attn_bv, L0_attn_Wo, L0_attn_bo)
    x = x + _L0_xattn_ref(_layernorm(x, axis=-1), ctx_1024, L0_xattn_wq, L0_xattn_bq, L0_xattn_wk, L0_xattn_bk, L0_xattn_wv, L0_xattn_bv, L0_xattn_wo, L0_xattn_bo)
    x = x + _L0_ffn_ref(_layernorm(x, axis=-1), L0_ffn_wg, L0_ffn_w1, L0_ffn_b1, L0_ffn_w2, L0_ffn_b2)
    x = x + _L1_attn_ref(_layernorm(x, axis=-1), L1_attn_Wq, L1_attn_Wk, L1_attn_Wv, L1_attn_Wo)
    x = x + _L1_xattn_ref(_layernorm(x, axis=-1), ctx_1024, ctx_1024, L1_xattn_Wq, L1_xattn_bq, L1_xattn_Wk, L1_xattn_bk, L1_xattn_Wv, L1_xattn_bv, L1_xattn_Wh, L1_xattn_bh)
    x = x + _L1_ffn_ref(_layernorm(x, axis=-1), L1_ffn_q_node_w, L1_ffn_q_node_b, L1_ffn_q_w1, L1_ffn_q_b1, L1_ffn_q_w2, L1_ffn_q_b2, L1_ffn_k_node_w, L1_ffn_k_node_b, L1_ffn_k_w1, L1_ffn_k_b1, L1_ffn_k_w2, L1_ffn_k_b2, L1_ffn_v_node_w, L1_ffn_v_node_b, L1_ffn_v_w1, L1_ffn_v_b1, L1_ffn_v_w2, L1_ffn_v_b2)
    return x

_drawn_inputs = setup_inputs


def setup_inputs(seed=0):
    import zlib

    import numpy as np

    out = dict(_drawn_inputs(seed))
    spreads = {'L0_attn_bq': (0.0, 0.295),
     'L0_attn_bk': (0.0, 0.1),
     'L0_attn_bv': (0.0, 0.1),
     'L0_attn_bo': (0.0, 0.1),
     'L0_xattn_bq': (0.0, 0.1),
     'L0_xattn_bk': (0.0, 0.8),
     'L0_xattn_bv': (0.0, 0.1),
     'L0_xattn_bo': (0.0, 0.1),
     'L0_ffn_b1': (0.0, 0.419),
     'L0_ffn_b2': (0.0, 0.303),
     'L1_xattn_bq': (0.0, 0.521),
     'L1_xattn_bk': (0.0, 0.8),
     'L1_xattn_bv': (0.0, 0.1),
     'L1_xattn_bh': (0.0, 0.1),
     'L1_ffn_q_b1': (0.0, 0.8),
     'L1_ffn_q_b2': (0.0, 0.8),
     'L1_ffn_k_b1': (0.0, 0.8),
     'L1_ffn_k_b2': (0.0, 0.8),
     'L1_ffn_v_b1': (0.0, 0.572),
     'L1_ffn_v_b2': (0.0, 0.37)}
    factors = {'L1_ffn_q_node_w': 6.606,
     'L1_ffn_q_node_b': 8.0,
     'L1_ffn_q_w1': 7.794,
     'L1_ffn_q_w2': 6.574,
     'L1_ffn_k_node_w': 6.653,
     'L1_ffn_k_node_b': 8.0,
     'L1_ffn_k_w1': 7.413,
     'L1_ffn_k_w2': 6.571,
     'L1_ffn_v_node_b': 4.44}
    for name, (base, spread) in spreads.items():
        noise = np.random.default_rng([zlib.crc32(name.encode()), seed]).standard_normal(out[name].shape)
        drawn = base * np.exp(spread * noise) if base else spread * noise
        out[name] = jnp.asarray(drawn.astype(out[name].dtype))
    for name, factor in factors.items():
        out[name] = (out[name] * factor).astype(out[name].dtype)
    return out
```

```python
from contextlib import ExitStack

import concourse.bass as bass
from concourse import mybir

F32 = mybir.dt.float32
BF16 = mybir.dt.bfloat16
U32 = mybir.dt.uint32
ALU = mybir.AluOpType
ACT = mybir.ActivationFunctionType
AX = mybir.AxisListType

P = 128
B, S, D = 2, 1024, 256
N = B * S
NT = N // P
KD = D // P
H, DH = 16, 16
G = H // 4
L = 77
CH = 512
NCH = N // CH
EPS = 1e-5
E_, C_, F_ = 8, N // 8, 1024
NLEAF, LEAFW, NNODE = 16, 64, 15
VW = DH + 1
VROW = H * VW + 15
STACK = 96
QPART = (0, 0, 1, 1, 0, 2)
KPART = (0, 1, 0, 1, 2, 0)
NEG = -1e30
ROUND = 12582912.0
QMAX = 7.0
THRESH = 0.05
UPTO = 6


class Stage:

    def __init__(self, name, keys, ternary=False, rope=False, quant=False, bias=True, mixed=False, index=0):
        self.name, self.keys, self.ternary, self.rope = name, keys, ternary, rope
        self.quant, self.bias, self.index = quant, bias, index
        self.mixed = mixed
        self.cross = keys == L
        self.ktiles = 1 if self.cross else keys // P
        self.krows = L if self.cross else P
        self.steps = self.ktiles * (S // CH)
        self.kch = 1 if self.cross else keys // CH
        items, late = [], []
        for gi in range(B * G):
            n = 0
            for qt in range(S // P):
                for j in range(1 if self.cross else 4):
                    for kc in range(self.kch):
                        items.append(("m", gi, qt, j, kc))
                        n += 1
                        if n == 3 and late:
                            items.append(late.pop())
            late.append(("t", gi))
        items.append(late.pop())
        self.items = items
        self.per_group = (S // P) * (1 if self.cross else 4) * self.kch
        self.t_at = {it[1]: n for n, it in enumerate(items) if it[0] == "t"}
        self.m_end = {}
        for n, it in enumerate(items):
            if it[0] == "m":
                self.m_end[it[1]] = n
        self.m_before = []
        c = 0
        for it in items:
            self.m_before.append(c)
            c += it[0] == "m"

    def lead(self, step):
        per = self.per_group + 1
        first = per + 5 + (0 if self.cross else 12)
        return min(len(self.items), first + ((step + 1) * per) // self.steps)


SELF0 = Stage("self0", S, ternary=True, quant=True, index=0)
CROSS0 = Stage("cross0", L, index=1)
SELF1 = Stage("self1", S, rope=True, bias=False, index=3)
CROSS1 = Stage("cross1", L, mixed=True, index=4)
ATTN = (SELF0, CROSS0, SELF1, CROSS1)


def units(a):
    out = [("k", 0, hh, 0, B * L) for hh in range(KD)] if a.cross else []
    for b in range(B):
        for hh in range(KD):
            for which in "q" if a.cross else "qk":
                out += [(which, b, hh, b * S + c, CH) for c in range(0, S, CH)]
    return out


def pool_marks(a):
    return 4 if a.index < 2 else 8


def weight_loads(a):
    return 4 + 4 * a.bias + a.cross + 2 * a.rope


def step_counts(a):
    nu, tiles, steps, groups = len(units(a)), B if a.cross else NT, B * G * a.steps, B * G
    c = {
        "w": 16 * weight_loads(a), "pj": nu, "pj_act": nu, "split": nu, "hi": 0 if a.rope else nu,
        "pj_rot": nu * a.rope, "pj_roped": nu * a.rope, "st0": 16 * ((nu + 1) // 2), "st1": 16 * (nu // 2),
        "vpj": tiles, "vev": tiles, "sc": 2 * steps, "ex": 2 * steps, "pv": steps, "oev": B * G * (S // CH),
        "mi": len(a.items), "mfree": len(a.items), "mxr": 0 if a.cross else groups, "rows": groups,
        "tern_sum": 2 * a.ternary, "tern_tot": 2 * a.ternary, "wready": 1 * a.ternary,
        "ymax": 1 * a.quant, "ygmax": 1 * a.quant,
    }
    for i in range(3):
        used = len(range(i, groups, 3))
        c[f"ldk{i}"], c[f"rl{i}"] = 16 * 12 * used, 16 * 3 * used
    for n in ("otp", "ocx", "ctp", "cev", "yp", "yev"):
        c[n] = NT
    return c


def decoder_kernel(nc, d, out, upto=UPTO):
    ctx = ExitStack()
    with ctx:
        def sb(name, shape, dt=F32):
            return ctx.enter_context(nc.sbuf_tensor(name, shape, dt))

        def sem(name):
            return ctx.enter_context(nc.semaphore(name))

        x = sb("x", [P, NT, D])
        norm = sb("norm", [P, 2 * NT * D])
        xn = norm[:, 0:NT * D].rearrange("p (t n) -> p t n", t=NT)
        xn_t = norm[:, NT * D:].rearrange("p (k n) -> p k n", k=KD)
        o_t = norm[:, :].rearrange("p (g n) -> p g n", g=G)
        ident = sb("ident", [P, P])
        rot = sb("rot", [P, P])
        ones = sb("ones", [P, P])
        ones_b = sb("ones_b", [P, P], BF16)
        tri_b = sb("tri_b", [P, P], BF16)
        stats = sb("stats", [P, NT, 6])
        mv = sb("mv", [P, NT, 2])
        ve = sb("ve", [P, NT])
        sd = sb("sd", [P, NT])
        rstd = sb("rstd", [P, NT])
        tmp_r = sb("tmp_r", [P, NT])
        y_max = sb("y_max", [P, 4])
        tri_f = sb("tri_f", [P, P])
        rev8_c = sb("rev8_c", [P, NT * E_])
        rev8 = rev8_c[:, :].rearrange("p (t e) -> p t e", t=NT)
        AW = 36864
        arena = sb("arena", [P, AW])
        top = [0]

        def cut(words, dt=F32):
            a = arena[:, top[0]:top[0] + words]
            top[0] += words
            assert top[0] <= AW, top[0]
            return a if dt == F32 else a.bitcast(dt)

        wq = cut(KD * D).rearrange("p (k n) -> p k n", k=KD)
        wk = cut(KD * D).rearrange("p (k n) -> p k n", k=KD)
        wv = cut(KD * D).rearrange("p (k n) -> p k n", k=KD)
        wo = cut(KD * D).rearrange("p (k n) -> p k n", k=KD)
        w_of = {"q": wq, "k": wk, "v": wv, "o": wo}
        bq = cut(KD)
        bk = cut(KD)
        bv = cut(D)
        bo = cut(D)
        ctx_t = cut(KD * B * L).rearrange("p (k n) -> p k n", k=KD)
        cos_t = cut(S)
        sin_t = cut(S)
        q_stack = [cut(4 * S // 2, BF16).rearrange("p (j n) -> p j n", j=4) for _ in range(3)]
        k_stack = [cut(4 * S // 2, BF16).rearrange("p (j n) -> p j n", j=4) for _ in range(3)]
        va = cut(NT * VROW).rearrange("p (t n) -> p t n", t=NT)
        probs = [cut(4 * CH).rearrange("p (j n) -> p j n", j=4) for _ in range(2)]
        proj = [cut(CH) for _ in range(2)]
        rest = [cut(CH) for _ in range(2)]
        roped = [cut(CH) for _ in range(2)]
        parts = [cut(3 * CH // 2, BF16).rearrange("p (s n) -> p s n", s=3) for _ in range(2)]
        mx_raw = cut(2 * 32).rearrange("p (k n) -> p k n", k=2)
        mx = cut(2 * 32).rearrange("p (k n) -> p k n", k=2)
        row_rest = cut(P)
        row_parts = cut(2 * 3 * P // 2, BF16).rearrange("p (a s n) -> p a s n", a=2, s=3)
        rec = [cut(H) for _ in range(2)]
        ctxn = [cut(D) for _ in range(2)]
        ctxn_t = [cut(D).rearrange("p (k n) -> p k n", k=KD) for _ in range(2)]
        top[0] = 4 * KD * D + 2 * KD + 2 * D + KD * B * L + 2 * S
        tern_top = top[0]
        y_all = cut(NT * D).rearrange("p (t n) -> p t n", t=NT)
        ctx_rows = y_all
        top[0] = tern_top
        w_abs = cut(KD * D)
        w_pos = cut(KD * D)
        w_neg = cut(KD * D)
        tern_s = cut(8)
        tern_d = cut(4)
        tern_n = cut(4)
        tern_a = cut(4)
        tern_c = cut(4)
        top[0] = 0
        ff_bias = cut(E_ * F_ // P)
        b2_all = cut(E_ * D).rearrange("p (e n) -> p e n", e=E_)
        wg = cut(KD * E_).rearrange("p (k n) -> p k n", k=KD)
        gl = cut(NT * E_).rearrange("p (t e) -> p t e", t=NT)
        gm = cut(NT * E_).rearrange("p (t e) -> p t e", t=NT)
        gt = cut(NT * E_).rearrange("p (t e) -> p t e", t=NT)
        onehot = cut(NT * E_).rearrange("p (t e) -> p t e", t=NT)
        before = (NT - 1) * E_
        onehot_pad = cut((before + NT * E_) // 2, BF16)
        onehot_b = onehot_pad[:, before:].rearrange("p (t e) -> p t e", t=NT)
        g_max = cut(NT)
        g_sum = cut(NT)
        g_rec = cut(NT)
        g_first = cut(NT)
        g_pos = cut(NT)
        g_keep = cut(NT)
        g_val = cut(NT)
        g_off = cut(NT)
        g_slot = cut(NT)
        slot_put = cut(NT, U32)
        slot_get = cut(NT, U32)
        g_back = cut(NT)
        w1e = [cut(KD * F_).rearrange("p (k n) -> p k n", k=KD) for _ in range(3)]
        w2e = [cut((F_ // P) * D).rearrange("p (k n) -> p k n", n=D) for _ in range(3)]
        disp = [cut(2 * D).rearrange("p (s n) -> p s n", s=2) for _ in range(2)]
        disp_t = [cut(KD * C_).rearrange("p (k n) -> p k n", k=KD) for _ in range(2)]
        hid = [cut((F_ // P) * C_).rearrange("p (k n) -> p k n", n=C_) for _ in range(2)]
        eo = [cut(2 * D).rearrange("p (s n) -> p s n", s=2) for _ in range(2)]
        back = cut(NT * D).rearrange("p (t n) -> p t n", t=NT)
        zero = back
        top[0] = 0
        nodes = cut(KD * 48).rearrange("p (k n) -> p k n", k=KD)
        node_b = cut(48)
        go = cut(NT * 48).rearrange("p (t n) -> p t n", t=NT)
        path = [cut(NT * 3 * (2 << n)).rearrange("p (a n) -> p a n", n=2 << n) for n in range(3)]
        sel = cut(NT * 96).rearrange("p (t n) -> p t n", t=NT)
        sel_t = cut(N)
        nsel_t = cut(N // 2, BF16)
        leaf_f = cut(F_)
        leaf_b = [cut(F_ // 2, BF16) for _ in range(3)]
        fb1 = cut(3 * (F_ // P)).rearrange("p (i n) -> p i n", i=3)
        fb2 = cut(3 * D).rearrange("p (i n) -> p i n", i=3)
        fw1 = [cut(KD * F_).rearrange("p (k n) -> p k n", k=KD) for _ in range(2)]
        fw2 = [cut((F_ // P) * D).rearrange("p (k n) -> p k n", n=D) for _ in range(2)]
        fh = cut((F_ // P) * CH).rearrange("p (k n) -> p k n", n=CH)
        fq_t = cut(KD * N).rearrange("p (k n) -> p k n", k=KD)
        fk_t = cut(KD * N).rearrange("p (k n) -> p k n", k=KD)
        fv = cut(NT * D).rearrange("p (t n) -> p t n", t=NT)
        f_mx = cut(NT)
        f_nmx = cut(NT)
        f_sum = cut(NT)
        f_rec = cut(NT)
        f_p = [fw1[0].rearrange("p k n -> p (k n)")[:, 0:S], fw1[0].rearrange("p k n -> p (k n)")[:, S:2 * S]]
        f_pt = [fw2[0].rearrange("p k n -> p (k n)")[:, 0:S].rearrange("p (k n) -> p k n", n=P),
                fw2[0].rearrange("p k n -> p (k n)")[:, S:2 * S].rearrange("p (k n) -> p k n", n=P)]

        ps = ctx.enter_context(nc.psum_tensor("ps", [P, 8, CH], F32))

        def dram(name, shape, dt=F32):
            return nc.dram_tensor(name, shape, dt, kind="Internal").ap()

        q_parts = [dram(f"q_parts{a.index}", [3, D, N], BF16) for a in ATTN]
        k_parts = [dram(f"k_parts{a.index}", [3, D, B * a.keys], BF16) for a in ATTN]
        x_d = dram("x_d", [N, D])
        x_mixed_d = dram("x_mixed_d", [N, D])
        disp_d = dram("disp_d", [N, D])
        eo_d = dram("eo_d", [N, D])

        s_const = sem("s_const")
        s_x = sem("s_x")
        s_castc = sem("s_castc")
        s_xmix = sem("s_xmix")
        s_xback = sem("s_xback")
        s_pool0 = sem("s_pool0")
        ev = sem("dve_order")
        ea = sem("act_order")
        nv = [0]
        na = [0]

        def vlink(v, ins):
            nv[0] += 1
            ins.then_inc(ev, 1)
            v.wait_ge(ev, nv[0])

        def alink(a, ins):
            na[0] += 1
            ins.then_inc(ea, 1)
            a.wait_ge(ea, na[0])

        def per_stage(*names):
            return {n: [sem(f"{n}{i}") for i in range(6)] for n in names}

        s_ln = per_stage("ln_var", "ln_sd", "ln_xn", "ln_tp", "ln_ev")
        s = {n: sem("attn_" + n) for n in step_counts(SELF0)}
        m = {n: sem("moe_" + n) for n in (
            "w", "lg", "ex_in", "ex", "oh", "cum", "slots", "zero", "zeroed", "put", "w1_0", "w1_1", "w1_2", "dl0", "dl1",
            "tp", "dt", "h", "hev", "y", "yev", "get", "b2", "st0", "st1", "xadd")}
        f = {n: sem("fff_" + n) for n in (
            "w", "nd", "ndev", "sel", "tp", "selt", "nselt", "wl0", "wl1", "h", "hev", "y", "yev", "sc", "mx", "ex",
            "ptp", "ptev", "ptev_v", "o", "oev", "leafc")}
        s_out = sem("s_out")

        AT, base = {}, {n: 0 for n in s}
        for a, qp, kp in zip(ATTN, q_parts, k_parts):
            AT[a.index] = (a, s, dict(base), qp, kp)
            base = {n: v + step_counts(a)[n] for n, v in base.items()}

        def scalar_done(eng, n):
            if n in AT:
                eng.wait_ge(s["cev"], AT[n][2]["cev"] + NT)
            elif n == 2:
                eng.wait_ge(m["hev"], E_ * F_ // P)

        block = ctx.enter_context(nc.Block())

        @block.tensor
        def _(pe):
            def layer_norm(n):
                for u in range(NT // 2):
                    pe.wait_ge(s_ln["ln_xn"][n], 2 * u + 2)
                    if u >= 2:
                        pe.wait_ge(s_ln["ln_ev"][n], u - 1)
                    for k in range(KD):
                        for t in range(2):
                            mm = pe.transpose(ps[:, u % 2, (k * 2 + t) * P:(k * 2 + t + 1) * P],
                                              xn[:, 2 * u + t, k * P:(k + 1) * P], ident[:, :])
                    mm.then_inc(s_ln["ln_tp"][n], 1)

            def attention(a, s, o):
                if a.ternary:
                    pe.wait_ge(s["tern_sum"], o["tern_sum"] + 1)
                    pe.matmul(ps[:, 7, 0:4], ones[:, :], tern_s[:, 0:4], start=True, stop=True).then_inc(s["tern_tot"], 1)
                    pe.wait_ge(s["tern_sum"], o["tern_sum"] + 2)
                    pe.matmul(ps[:, 7, 8:16], ones[:, :], tern_s[:, 0:8], start=True, stop=True).then_inc(s["tern_tot"], 1)
                if a.ternary:
                    pe.wait_ge(s["wready"], o["wready"] + 1)
                pe.wait_ge(s["w"], o["w"] + 16 * weight_loads(a))
                pe.wait_ge(s_ln["ln_ev"][a.index], NT // 2)
                for u, (which, b, hh, c, w) in enumerate(units(a)):
                    if u >= 2:
                        pe.wait_ge(s["pj_act"], o["pj_act"] + u - 1)
                    src = xn_t if which == "q" else (ctx_t if a.cross else xn_t)
                    for k in range(KD):
                        mm = pe.matmul(ps[:, u % 2, 0:w], w_of[which][:, k, hh * P:(hh + 1) * P],
                                       src[:, k, c:c + w], start=(k == 0), stop=(k == KD - 1))
                    mm.then_inc(s["pj"], 1)
                    if a.rope and u >= 1:
                        rotate(a, s, o, u - 1)
                if a.rope:
                    rotate(a, s, o, len(units(a)) - 1)
                nv_t = B if a.cross else NT
                for t in range(nv_t):
                    if t >= 2:
                        pe.wait_ge(s["vev"], o["vev"] + t - 1)
                    for k in range(KD):
                        lhs = ctx_t[:, k, t * L:(t + 1) * L] if a.cross else xn_t[:, k, t * P:(t + 1) * P]
                        mm = pe.matmul(ps[0:a.krows, 4 + t % 2, 0:D], lhs, wv[:, k, :],
                                       start=(k == 0), stop=(k == KD - 1))
                    mm.then_inc(s["vpj"], 1)
                pe.wait_ge(s["vev"], o["vev"] + nv_t)
                pe.wait_ge(s["pj_act"], o["pj_act"] + len(units(a)))
                if a.rope:
                    pe.wait_ge(s["pj_roped"], o["pj_roped"] + len(units(a)))
                pe.wait_ge(s_pool0, pool_marks(a))

                done = [0]

                def max_items(upto_):
                    while done[0] < upto_:
                        n = done[0]
                        it = a.items[n]
                        gi = it[1]
                        if n >= 3:
                            pe.wait_ge(s["mfree"], o["mfree"] + n - 2)
                        bank = 5 + n % 3
                        if it[0] == "t":
                            if a.cross:
                                pe.wait_ge(s["mfree"], o["mfree"] + a.m_end[gi] + 1)
                            else:
                                pe.wait_ge(s["mxr"], o["mxr"] + gi + 1)
                            mm = pe.transpose(ps[0:32, bank, 0:P], mx[:, gi % 2, :], ident[:, :])
                        else:
                            _, _, qt, j, kc = it
                            if a.m_end.get(gi - 1, -1) < n and (qt, j, kc) == (0, 0, 0):
                                pe.wait_ge(s[f"ldk{gi % 3}"], o[f"ldk{gi % 3}"] + 16 * 12 * (gi // 3 + 1))
                            if a.cross:
                                for j in range(4):
                                    mm = pe.matmul(ps[:, bank, j * L:(j + 1) * L],
                                                   q_stack[gi % 3][0:STACK, j, qt * P:(qt + 1) * P],
                                                   k_stack[gi % 3][0:STACK, j, 0:L], start=True, stop=True)
                            else:
                                mm = pe.matmul(ps[:, bank, :], q_stack[gi % 3][0:STACK, j, qt * P:(qt + 1) * P],
                                               k_stack[gi % 3][0:STACK, j, kc * CH:(kc + 1) * CH],
                                               start=True, stop=True)
                        mm.then_inc(s["mi"], 1)
                        done[0] += 1

                def values(n):
                    gi, r = divmod(n, a.steps)
                    qc, kt = divmod(r, a.ktiles)
                    b, g = divmod(gi, G)
                    pe.wait_ge(s["ex"], o["ex"] + 2 * n + 2)
                    if kt == 0 and n:
                        pe.wait_ge(s["oev"], o["oev"] + n // a.ktiles)
                    for j in range(4):
                        t = b if a.cross else b * (S // P) + kt
                        h = 4 * g + j
                        mm = pe.matmul(ps[32 * j:32 * j + 32, 4, :], va[0:a.krows, t, h * VW:h * VW + 32],
                                       probs[n % 2][0:a.krows, j, :], start=(kt == 0), stop=(kt == a.ktiles - 1),
                                       tile_position=(0, 32 * j))
                    mm.then_inc(s["pv"], 1)

                max_items(a.lead(-1))
                total = B * G * a.steps
                for n in range(total):
                    gi, r = divmod(n, a.steps)
                    qc, kt = divmod(r, a.ktiles)
                    if r == 0:
                        pe.wait_ge(s[f"rl{gi % 3}"], o[f"rl{gi % 3}"] + 16 * 3 * (gi // 3 + 1))
                    for pr in range(2):
                        e = 2 * n + pr
                        if e >= 2:
                            pe.wait_ge(s["ex"], o["ex"] + e - 1)
                        for j in (2 * pr, 2 * pr + 1):
                            mm = pe.matmul(ps[0:a.krows, 2 * pr + j % 2, :],
                                           k_stack[gi % 3][0:STACK + 3, j, kt * P:kt * P + a.krows],
                                           q_stack[gi % 3][0:STACK + 3, j, qc * CH:(qc + 1) * CH],
                                           start=True, stop=True)
                        mm.then_inc(s["sc"], 1)
                    if n:
                        values(n - 1)
                    max_items(a.lead(n))
                values(total - 1)

                def turn(t):
                    if t == 0:
                        pe.wait_ge(s["oev"], o["oev"] + B * G * (S // CH))
                    if t >= 2:
                        pe.wait_ge(s["ocx"], o["ocx"] + t - 1)
                    for i in range(4):
                        if a.mixed:
                            g, place = t // 4, 4 * (t % 4) + i
                            src = o_t[:, g, :].rearrange("p (r m) -> p r m", m=H)[:, :, place]
                        else:
                            src = o_t[:, i, t * P:(t + 1) * P]
                        mm = pe.transpose(ps[:, t % 2, i * P:(i + 1) * P], src, ident[:, :])
                    mm.then_inc(s["otp"], 1)

                def turn_back(t):
                    pe.wait_ge(s["ocx"], o["ocx"] + (4 * (t // 4) + 4 if a.mixed else t + 1))
                    if t >= 2:
                        pe.wait_ge(s["cev"], o["cev"] + t - 1)
                    rows = ctx_rows[:, t, :] if a.mixed else ctxn[t % 2]
                    for k in range(KD):
                        mm = pe.transpose(ps[:, 2 + t % 2, k * P:(k + 1) * P], rows[:, k * P:(k + 1) * P],
                                          ident[:, :])
                    mm.then_inc(s["ctp"], 1)

                def project(t):
                    pe.wait_ge(s["cev"], o["cev"] + t + 1)
                    if t >= 2:
                        pe.wait_ge(s["yev"], o["yev"] + t - 1)
                    elif t == 0:
                        pe.wait_ge(s["mfree"], o["mfree"] + len(a.items))
                    for k in range(KD):
                        mm = pe.matmul(ps[:, 6 + t % 2, 0:D], ctxn_t[t % 2][:, k, :], wo[:, k, :],
                                       start=(k == 0), stop=(k == KD - 1))
                    mm.then_inc(s["yp"], 1)

                lag = 4 if a.mixed else 1
                for t in range(NT + lag + 1):
                    if t < NT:
                        turn(t)
                    if lag <= t < NT + lag:
                        turn_back(t - lag)
                    if t > lag:
                        project(t - lag - 1)

            def rotate(a, s, o, u):
                pe.wait_ge(s["pj_act"], o["pj_act"] + u + 1)
                if u >= 2:
                    pe.wait_ge(s["pj_roped"], o["pj_roped"] + u - 1)
                w = units(a)[u][4]
                pe.matmul(ps[:, 2 + u % 2, 0:w], rot[:, :], proj[u % 2][:, 0:w], start=True, stop=True)\
                  .then_inc(s["pj_rot"], 1)

            def experts():
                n = 2
                pe.wait_ge(s_ln["ln_ev"][n], NT // 2)
                pe.wait_ge(m["w"], 16)
                for t in range(NT):
                    for k in range(KD):
                        mm = pe.matmul(ps[:, 4, t * E_:(t + 1) * E_], xn_t[:, k, t * P:(t + 1) * P], wg[:, k, :],
                                       start=(k == 0), stop=(k == KD - 1))
                mm.then_inc(m["lg"], 1)
                pe.wait_ge(m["oh"], 1)
                for k in range(NT):
                    mm = pe.matmul(ps[:, 5, 0:NT * E_], (ones_b if k else tri_b)[:, :],
                                   onehot_pad[:, before - k * E_:before - k * E_ + NT * E_],
                                   start=(k == 0), stop=(k == NT - 1))
                mm.then_inc(m["cum"], 1)

                def turn(e):
                    pe.wait_ge(m[f"dl{e % 2}"], 16 * (e // 2 + 1))
                    if e:
                        pe.wait_ge(m["dt"], e)
                    for k in range(KD):
                        for c in range(2):
                            mm = pe.transpose(ps[:, 0, k * C_ + c * P:k * C_ + (c + 1) * P],
                                              disp[e % 2][:, c, k * P:(k + 1) * P], ident[:, :])
                    mm.then_inc(m["tp"], 1)

                turn(0)
                for e in range(E_):
                    pe.wait_ge(m["dt"], e + 1)
                    pe.wait_ge(m[f"w1_{e % 3}"], 32 * (e // 3 + 1))
                    for ht in range(F_ // P):
                        u = e * (F_ // P) + ht
                        if u >= 3:
                            pe.wait_ge(m["hev"], u - 2)
                        for k in range(KD):
                            mm = pe.matmul(ps[:, 1 + u % 3, 0:C_], w1e[e % 3][:, k, ht * P:(ht + 1) * P],
                                           disp_t[e % 2][:, k, :], start=(k == 0), stop=(k == KD - 1))
                        mm.then_inc(m["h"], 1)
                    if e + 1 < E_:
                        turn(e + 1)
                    pe.wait_ge(m["hev"], (e + 1) * (F_ // P))
                    for c in range(2):
                        v = 2 * e + c
                        if v >= 2:
                            pe.wait_ge(m["yev"], v - 1)
                        for ht in range(F_ // P):
                            mm = pe.matmul(ps[:, 6 + v % 2, 0:D], hid[e % 2][:, ht, c * P:(c + 1) * P],
                                           w2e[e % 3][:, ht, :], start=(ht == 0), stop=(ht == F_ // P - 1))
                        mm.then_inc(m["y"], 1)

            def leaves():
                n = 5
                pe.wait_ge(s_ln["ln_ev"][n], NT // 2)
                pe.wait_ge(f["w"], 16 * 6)
                for t in range(NT):
                    for k in range(KD):
                        mm = pe.matmul(ps[:, 2 + t // 8, (t % 8) * 48:(t % 8) * 48 + 48],
                                       xn_t[:, k, t * P:(t + 1) * P], nodes[:, k, :],
                                       start=(k == 0), stop=(k == KD - 1))
                mm.then_inc(f["nd"], 1)
                pe.wait_ge(f["sel"], 1)
                for u in range(NT // 4):
                    if u >= 2:
                        pe.wait_ge(f["selt"], u - 1)
                        pe.wait_ge(f["nselt"], u - 1)
                    for t in range(4):
                        mm = pe.transpose(ps[0:96, 4 + u % 2, t * P:(t + 1) * P], sel[:, 4 * u + t, :], ident[:, :])
                    mm.then_inc(f["tp"], 1)
                pe.wait_ge(f["selt"], NT // 4)
                pe.wait_ge(f["nselt"], NT // 4)
                pe.wait_ge(f["ndev"], 3)
                hu = yu = 0
                for i in range(3):
                    pe.wait_ge(f[f"wl{i % 2}"], 32 * (i // 2 + 1))
                    for c in range(NCH):
                        for ht in range(F_ // P):
                            if hu >= 3:
                                pe.wait_ge(f["hev"], hu - 2)
                            o = ps[:, 5 + hu % 3, :]
                            for k in range(KD):
                                pe.matmul(o, fw1[i % 2][:, k, ht * P:(ht + 1) * P],
                                          xn_t[:, k, c * CH:(c + 1) * CH], start=(k == 0), stop=False)
                            pe.matmul(o, leaf_b[i][0:96, ht * P:(ht + 1) * P], nsel_t[0:96, c * CH:(c + 1) * CH],
                                      start=False, stop=True).then_inc(f["h"], 1)
                            hu += 1
                        pe.wait_ge(f["hev"], hu)
                        if i < 2:
                            for k in range(KD):
                                if yu >= 2:
                                    pe.wait_ge(f["yev"], yu - 1)
                                o = ps[:, yu % 2, :]
                                for ht in range(F_ // P):
                                    pe.matmul(o, fw2[i % 2][:, ht, k * P:(k + 1) * P], fh[:, ht, :],
                                              start=(ht == 0), stop=False)
                                pe.matmul(o, fb2[0:96, i, k * P:(k + 1) * P], sel_t[0:96, c * CH:(c + 1) * CH],
                                          start=False, stop=True).then_inc(f["y"], 1)
                                yu += 1
                        else:
                            for t in range(4):
                                if yu >= 2:
                                    pe.wait_ge(f["yev"], yu - 1)
                                o = ps[:, yu % 2, 0:D]
                                for ht in range(F_ // P):
                                    pe.matmul(o, fh[:, ht, t * P:(t + 1) * P], fw2[i % 2][:, ht, :],
                                              start=(ht == 0), stop=False)
                                pe.matmul(o, sel_t[0:96, c * CH + t * P:c * CH + (t + 1) * P], fb2[0:96, i, :],
                                          start=False, stop=True).then_inc(f["y"], 1)
                                yu += 1
                pe.wait_ge(f["yev"], yu)

                def scores(t):
                    if t >= 2:
                        pe.wait_ge(f["ex"], t - 1)
                    for kc in range(2):
                        for k in range(KD):
                            mm = pe.matmul(ps[:, 2 * (t % 2) + kc, :], fq_t[:, k, t * P:(t + 1) * P],
                                           fk_t[:, k, (t // 8) * S + kc * CH:(t // 8) * S + (kc + 1) * CH],
                                           start=(k == 0), stop=(k == KD - 1))
                    mm.then_inc(f["sc"], 1)

                def turn(t):
                    pe.wait_ge(f["ex"], t + 1)
                    if t:
                        pe.wait_ge(f["ptev"], t)
                        pe.wait_ge(f["ptev_v"], t)
                    for kt in range(S // P):
                        mm = pe.transpose(ps[:, 4 + kt // 4, (kt % 4) * P:(kt % 4 + 1) * P],
                                          f_p[t % 2][:, kt * P:(kt + 1) * P], ident[:, :])
                    mm.then_inc(f["ptp"], 1)

                def values(t):
                    pe.wait_ge(f["ptev"], t + 1)
                    pe.wait_ge(f["ptev_v"], t + 1)
                    if t >= 2:
                        pe.wait_ge(f["oev"], t - 1)
                    for kt in range(S // P):
                        mm = pe.matmul(ps[:, 6 + t % 2, 0:D], f_pt[t % 2][:, kt, :], fv[:, (t // 8) * 8 + kt, :],
                                       start=(kt == 0), stop=(kt == S // P - 1))
                    mm.then_inc(f["o"], 1)

                scores(0)
                for t in range(NT):
                    if t + 1 < NT:
                        scores(t + 1)
                    turn(t)
                    if t:
                        values(t - 1)
                values(NT - 1)

            pe.wait_ge(s_const, 16 * 5)
            pe.wait_ge(s_castc, 1)
            for n in range(upto):
                if n:
                    scalar_done(pe, n - 1)
                layer_norm(n)
                if n in AT:
                    a, s, o, _, _ = AT[n]
                    attention(a, s, o)
                elif n == 2:
                    experts()
                else:
                    leaves()

        @block.scalar
        def _(act):
            def layer_norm(n):
                act.wait_ge(s_ln["ln_var"][n], 1)
                act.activation(sd[:, :], ve[:, :], ACT.Sqrt).then_inc(s_ln["ln_sd"][n], 1)
                for u in range(NT // 2):
                    act.wait_ge(s_ln["ln_tp"][n], u + 1)
                    bank = ps[:, u % 2, :].rearrange("p (k n) -> p k n", k=KD)
                    if n == 5:
                        for k in range(KD):
                            ins = act.activation(
                                xn_t[:, k, :].rearrange("p (b t r) -> p t b r", b=B, r=64)[:, 2 * u:2 * u + 2],
                                bank[:, k, :].rearrange("p (t b r) -> p t b r", t=2, b=B), ACT.Copy)
                        ins.then_inc(s_ln["ln_ev"][n], 1)
                        continue
                    act.activation(xn_t[:, :, 2 * u * P:(2 * u + 2) * P], bank, ACT.Copy)\
                       .then_inc(s_ln["ln_ev"][n], 1)

            def attention(a, s, o):
                act.wait_ge(s["w"], o["w"] + 16 * weight_loads(a))
                for u, (which, b, hh, c, w) in enumerate(units(a)):
                    act.wait_ge(s["pj"], o["pj"] + u + 1)
                    if u >= 2:
                        act.wait_ge(s["split"], o["split"] + u - 1)
                    if a.rope:
                        if u >= 2:
                            act.wait_ge(s["pj_roped"], o["pj_roped"] + u - 1)
                        act.activation(proj[u % 2][:, 0:w], ps[:, u % 2, 0:w], ACT.Copy).then_inc(s["pj_act"], 1)
                    else:
                        bias = (bq if which == "q" else bk)[:, hh:hh + 1]
                        if u >= 2:
                            act.wait_ge(s[f"st{u % 2}"], o[f"st{u % 2}"] + 16 * (u // 2))
                        act.activation(parts[u % 2][:, 0, 0:w], ps[:, u % 2, 0:w], ACT.Identity, bias=bias)\
                           .then_inc(s["hi"], 1)
                        act.activation(proj[u % 2][:, 0:w], ps[:, u % 2, 0:w], ACT.Identity, bias=bias)\
                           .then_inc(s["pj_act"], 1)
                total = B * G * a.steps
                scale = DH ** -0.5

                def copy_sums(i):
                    gi, qc = divmod(i, S // CH)
                    b, g = divmod(gi, G)
                    act.wait_ge(s["pv"], o["pv"] + (i + 1) * a.ktiles)
                    act.activation(o_t[:, g, b * S + qc * CH:b * S + (qc + 1) * CH], ps[:, 4, :], ACT.Copy)\
                       .then_inc(s["oev"], 1)

                for n in range(total):
                    if n >= 2:
                        act.wait_ge(s["pv"], o["pv"] + n - 1)
                    for pr in range(2):
                        act.wait_ge(s["sc"], o["sc"] + 2 * n + pr + 1)
                        act.activation(probs[n % 2][0:a.krows, 2 * pr:2 * pr + 2, :],
                                       ps[0:a.krows, 2 * pr:2 * pr + 2, :], ACT.Exp, scale=scale)\
                           .then_inc(s["ex"], 1)
                    if n and n % a.ktiles == 0:
                        copy_sums(n // a.ktiles - 1)
                copy_sums(total // a.ktiles - 1)
                for t in range(NT):
                    act.wait_ge(s["ctp"], o["ctp"] + t + 1)
                    if t >= 2:
                        act.wait_ge(s["yp"], o["yp"] + t - 1)
                    act.activation(ctxn_t[t % 2][:, :, :],
                                   ps[:, 2 + t % 2, 0:D].rearrange("p (k n) -> p k n", k=KD), ACT.Copy)\
                       .then_inc(s["cev"], 1)

            def experts():
                act.wait_ge(m["b2"], 32)
                act.wait_ge(m["ex_in"], 1)
                act.activation(gl[:, :, :], gm[:, :, :], ACT.Exp).then_inc(m["ex"], 1)
                for e in range(E_):
                    for ht in range(F_ // P):
                        u = e * (F_ // P) + ht
                        act.wait_ge(m["h"], u + 1)
                        if e >= 2 and ht == 0:
                            act.wait_ge(m["y"], 2 * (e - 1))
                        act.activation(hid[e % 2][:, ht, :], ps[:, 1 + u % 3, 0:C_], ACT.Relu,
                                       bias=ff_bias[:, u:u + 1]).then_inc(m["hev"], 1)

            def leaves():
                act.wait_ge(f["w"], 16 * 6)
                for u in range(NT // 4):
                    act.wait_ge(f["tp"], u + 1)
                    act.activation(sel_t[0:96, u * CH:(u + 1) * CH], ps[0:96, 4 + u % 2, :], ACT.Copy)\
                       .then_inc(f["selt"], 1)
                hu = yu = 0
                for i in range(3):
                    for c in range(NCH):
                        for ht in range(F_ // P):
                            act.wait_ge(f["h"], hu + 1)
                            if ht == 0 and yu:
                                act.wait_ge(f["y"], yu)
                            act.activation(fh[:, ht, :], ps[:, 5 + hu % 3, :], ACT.Relu, bias=fb1[:, i, ht:ht + 1])\
                               .then_inc(f["hev"], 1)
                            hu += 1
                        yu += 2 if i < 2 else 4
                for t in range(NT):
                    act.wait_ge(f["mx"], t + 1)
                    if t >= 2:
                        act.wait_ge(f["ptp"], t - 1)
                    act.activation(f_p[t % 2], ps[:, 2 * (t % 2):2 * (t % 2) + 2, :].rearrange("p a n -> p (a n)"),
                                   ACT.Exp, bias=f_nmx[:, t:t + 1], scale=D ** -0.5,
                                   accum_out=f_sum[:, t:t + 1]).then_inc(f["ex"], 1)
                    act.wait_ge(f["ptp"], t + 1)
                    if t >= 2:
                        act.wait_ge(f["o"], t - 1)
                    act.activation(f_pt[t % 2][:, 0:4, :], ps[:, 4, :].rearrange("p (k n) -> p k n", n=P), ACT.Copy)\
                       .then_inc(f["ptev"], 1)

            for n in range(upto):
                layer_norm(n)
                if n in AT:
                    a, s, o, _, _ = AT[n]
                    attention(a, s, o)
                elif n == 2:
                    experts()
                else:
                    leaves()

        @block.vector
        def _(dve):
            def stat(n, t):
                return dve.bn_stats(stats[:, t, :], x[:, t, :])

            def layer_norm(n):
                for t in range(NT):
                    last = dve.bn_aggr(mv[:, t, :], stats[:, t, :])
                vlink(dve, last)
                dve.tensor_scalar(ve[:, :], mv[:, :, 1], EPS, None, ALU.add).then_inc(s_ln["ln_var"][n], 1)
                dve.wait_ge(s_ln["ln_sd"][n], 1)
                vlink(dve, dve.reciprocal(rstd[:, :], sd[:, :]))
                vlink(dve, dve.tensor_tensor(tmp_r[:, :], rstd[:, :], rstd[:, :], ALU.mult))
                vlink(dve, dve.tensor_tensor(tmp_r[:, :], tmp_r[:, :], ve[:, :], ALU.mult))
                vlink(dve, dve.tensor_scalar(tmp_r[:, :], tmp_r[:, :], -0.5, 1.5, ALU.mult, ALU.add))
                vlink(dve, dve.tensor_tensor(rstd[:, :], rstd[:, :], tmp_r[:, :], ALU.mult))
                for t in range(NT):
                    dve.tensor_scalar(xn[:, t, :], x[:, t, :], mv[:, t, 0:1], rstd[:, t:t + 1],
                                      ALU.subtract, ALU.mult).then_inc(s_ln["ln_xn"][n], 1)

            def ternary(s, o):
                dve.wait_ge(s["w"], o["w"] + 16 * 8)
                ws = [w_of[c].rearrange("p k n -> p (k n)") for c in "qkvo"]
                for i, w in enumerate(ws):
                    last = dve.tensor_reduce(tern_s[:, i:i + 1], w, AX.X, ALU.add, apply_absolute_value=True)
                last.then_inc(s["tern_sum"], 1)
                dve.wait_ge(s["tern_tot"], o["tern_tot"] + 1)
                vlink(dve, dve.tensor_scalar(tern_d[:, :], ps[:, 7, 0:4], 1.0 / (D * D), THRESH, ALU.mult, ALU.mult))
                vlink(dve, dve.tensor_scalar(tern_n[:, :], tern_d[:, :], -1.0, None, ALU.mult))
                for i, w in enumerate(ws):
                    vlink(dve, dve.scalar_tensor_tensor(w_abs, w, -1.0, w, ALU.mult, ALU.max))
                    vlink(dve, dve.scalar_tensor_tensor(w_pos, w_abs, tern_d[:, i:i + 1], w_abs, ALU.is_gt, ALU.mult,
                                                        accum_out=tern_s[:, i:i + 1]))
                    vlink(dve, dve.tensor_scalar(w_neg, w_abs, tern_d[:, i:i + 1], None, ALU.is_gt))
                    last = dve.tensor_reduce(tern_s[:, 4 + i:5 + i], w_neg, AX.X, ALU.add)
                    if i < 3:
                        vlink(dve, last)
                last.then_inc(s["tern_sum"], 1)
                dve.wait_ge(s["tern_tot"], o["tern_tot"] + 2)
                vlink(dve, dve.tensor_scalar(tern_c[:, :], ps[:, 7, 12:16], 1.0, None, ALU.max))
                vlink(dve, dve.reciprocal(tern_a[:, :], tern_c[:, :]))
                vlink(dve, dve.tensor_tensor(tern_a[:, :], ps[:, 7, 8:12], tern_a[:, :], ALU.mult))
                for i, w in enumerate(ws):
                    dve.tensor_scalar(w_pos, w, tern_d[:, i:i + 1], tern_a[:, i:i + 1], ALU.is_gt, ALU.mult)
                    vlink(dve, dve.tensor_scalar(w_neg, w, tern_n[:, i:i + 1], tern_a[:, i:i + 1],
                                                 ALU.is_lt, ALU.mult))
                    vlink(dve, dve.tensor_tensor(w_pos, w_pos, w_neg, ALU.subtract))
                    vlink(dve, dve.tensor_tensor(w_pos, w_pos, w, ALU.subtract))
                    last = dve.tensor_tensor(w, w, w_pos, ALU.add)
                    if i < 3:
                        vlink(dve, last)
                last.then_inc(s["wready"], 1)

            def attention(a, s, o):
                if a.ternary:
                    ternary(s, o)
                else:
                    dve.wait_ge(s["w"], o["w"] + 16 * weight_loads(a))
                dve.wait_ge(s_pool0, pool_marks(a))
                for u, (which, b, hh, c, w) in enumerate(units(a)):
                    pt = parts[u % 2]
                    full = proj[u % 2][:, 0:w]
                    dve.wait_ge(s["pj_act"], o["pj_act"] + u + 1)
                    if a.rope:
                        c0 = c % S
                        dve.wait_ge(s["pj_rot"], o["pj_rot"] + u + 1)
                        if u >= 2:
                            dve.wait_ge(s[f"st{u % 2}"], o[f"st{u % 2}"] + 16 * (u // 2))
                        dve.tensor_tensor(roped[u % 2][:, 0:w], full, cos_t[:, c0:c0 + w], ALU.mult)
                        vlink(dve, dve.tensor_tensor(rest[u % 2][:, 0:w], ps[:, 2 + u % 2, 0:w],
                                                     sin_t[:, c0:c0 + w], ALU.mult))
                        full = roped[u % 2][:, 0:w]
                        ins = dve.tensor_tensor(full, full, rest[u % 2][:, 0:w], ALU.add)
                        ins.then_inc(s["pj_roped"], 1)
                        dve.wait_ge(s["pj_roped"], o["pj_roped"] + u + 1)
                        vlink(dve, dve.tensor_copy(pt[:, 0, 0:w], full))
                    else:
                        dve.wait_ge(s["hi"], o["hi"] + u + 1)
                    r = rest[u % 2][:, 0:w]
                    vlink(dve, dve.tensor_tensor(r, full, pt[:, 0, 0:w], ALU.subtract))
                    vlink(dve, dve.tensor_copy(pt[:, 1, 0:w], r))
                    dve.tensor_tensor(pt[:, 2, 0:w], r, pt[:, 1, 0:w], ALU.subtract).then_inc(s["split"], 1)
                for t in range(B if a.cross else NT):
                    dve.wait_ge(s["vpj"], o["vpj"] + t + 1)
                    dst = va[0:a.krows, t, 0:H * VW].rearrange("p (h n) -> p h n", n=VW)[:, :, 0:DH]
                    src = ps[0:a.krows, 4 + t % 2, 0:D].rearrange("p (h n) -> p h n", n=DH)
                    if a.bias:
                        ins = dve.tensor_tensor(dst, src, bv[0:a.krows, :].rearrange("p (h n) -> p h n", n=DH), ALU.add)
                    else:
                        ins = dve.tensor_copy(dst, src)
                    ins.then_inc(s["vev"], 1)
                for n, it in enumerate(a.items):
                    gi = it[1]
                    bank = 5 + n % 3
                    dve.wait_ge(s["mi"], o["mi"] + n + 1)
                    if it[0] == "m":
                        _, _, qt, j, kc = it
                        if a.cross:
                            dst = mx[:, gi % 2, :].rearrange("p (j q) -> p j q", j=4)[:, :, qt]
                            ins = dve.tensor_reduce(dst, ps[:, bank, 0:4 * L].rearrange("p (j n) -> p j n", j=4),
                                                    AX.X, ALU.max)
                        else:
                            ins = dve.tensor_reduce(mx_raw[:, kc, j * 8 + qt:j * 8 + qt + 1], ps[:, bank, :],
                                                    AX.X, ALU.max)
                        ins.then_inc(s["mfree"], 1)
                        if n == a.m_end[gi]:
                            if not a.cross:
                                dve.wait_ge(s["mfree"], o["mfree"] + n + 1)
                                dve.tensor_tensor(mx[:, gi % 2, :], mx_raw[:, 0, :], mx_raw[:, 1, :], ALU.max)\
                                   .then_inc(s["mxr"], 1)
                                dve.wait_ge(s["mxr"], o["mxr"] + gi + 1)
                    else:
                        rp = row_parts[0:32, gi % 2]
                        if gi >= 2:
                            dve.wait_ge(s[f"rl{(gi - 2) % 3}"], o[f"rl{(gi - 2) % 3}"] + 48 * ((gi - 2) // 3 + 1))
                        vlink(dve, dve.tensor_scalar(rp[:, 0, :], ps[0:32, bank, 0:P], -1.0, None, ALU.mult))
                        ins = dve.scalar_tensor_tensor(row_rest[0:32, :], ps[0:32, bank, 0:P], -1.0, rp[:, 0, :],
                                                       ALU.mult, ALU.subtract)
                        ins.then_inc(s["mfree"], 1)
                        dve.wait_ge(s["mfree"], o["mfree"] + n + 1)
                        vlink(dve, dve.tensor_copy(rp[:, 1, :], row_rest[0:32, :]))
                        dve.tensor_tensor(rp[:, 2, :], row_rest[0:32, :], rp[:, 1, :], ALU.subtract)\
                           .then_inc(s["rows"], 1)
                n_st = a.index

                def normalise(t):
                    dve.wait_ge(s["otp"], o["otp"] + t + 1)
                    view = ps[:, t % 2, :].rearrange("p (h n) -> p h n", n=32)
                    if a.mixed:
                        vlink(dve, dve.reciprocal(rec[t % 2][:, :], view[:, :, DH]))
                        rows = ctx_rows[:, 4 * (t // 4):4 * (t // 4) + 4, 4 * DH * (t % 4):4 * DH * (t % 4 + 1)]
                        for i in range(4):
                            ins = dve.tensor_tensor(rows[:, :, i * DH:(i + 1) * DH], view[:, 4 * i:4 * i + 4, 0:DH],
                                                    rec[t % 2][:, 4 * i:4 * i + 4].unsqueeze(2)
                                                    .broadcast_to([P, 4, DH]), ALU.mult)
                        ins.then_inc(s["ocx"], 1)
                        return
                    if t >= 2:
                        dve.wait_ge(s["ctp"], o["ctp"] + t - 1)
                    vlink(dve, dve.reciprocal(rec[t % 2][:, :], view[:, :, DH]))
                    dve.tensor_tensor(ctxn[t % 2].rearrange("p (h n) -> p h n", n=DH), view[:, :, 0:DH],
                                      rec[t % 2][:, :].unsqueeze(2).broadcast_to([P, H, DH]), ALU.mult)\
                       .then_inc(s["ocx"], 1)

                def finish(t):
                    dve.wait_ge(s["yp"], o["yp"] + t + 1)
                    y = ps[:, 6 + t % 2, 0:D]
                    if a.quant:
                        ins = dve.tensor_tensor(y_all[:, t, :], y, bo, ALU.add)
                        ins.then_inc(s["yev"], 1)
                        dve.wait_ge(s["yev"], o["yev"] + t + 1)
                        ins = dve.tensor_reduce(tmp_r[:, t:t + 1], y_all[:, t, :], AX.X, ALU.max,
                                                apply_absolute_value=True)
                        if t == NT - 1:
                            vlink(dve, ins)
                        return
                    if a.bias:
                        vlink(dve, dve.tensor_tensor(x[:, t, :], x[:, t, :], bo, ALU.add))
                    dve.tensor_tensor(x[:, t, :], x[:, t, :], y, ALU.add).then_inc(s["yev"], 1)
                    dve.wait_ge(s["yev"], o["yev"] + t + 1)
                    if t < NT - 1:
                        stat(n_st + 1, t)
                    else:
                        vlink(dve, stat(n_st + 1, t))

                if a.mixed:
                    dve.wait_ge(s_xmix, 48)
                lag = 5 if a.mixed else 2
                for t in range(NT + lag):
                    if t < NT:
                        normalise(t)
                    if t >= lag:
                        finish(t - lag)
                if a.quant:
                    quantise(s, o)

            def quantise(s, o):
                dve.tensor_reduce(y_max[:, 0:1], tmp_r[:, :], AX.X, ALU.max).then_inc(s["ymax"], 1)
                dve.wait_ge(s["ygmax"], o["ygmax"] + 1)
                vlink(dve, dve.tensor_scalar(y_max[:, 2:3], y_max[:, 1:2], 1.0 / QMAX, 1e-8, ALU.mult, ALU.max))
                vlink(dve, dve.reciprocal(y_max[:, 3:4], y_max[:, 2:3]))
                for t in range(NT):
                    y, z = y_all[:, t, :], xn[:, t, :]
                    vlink(dve, dve.tensor_scalar(z, y, y_max[:, 3:4], ROUND, ALU.mult, ALU.add))
                    vlink(dve, dve.tensor_scalar(z, z, -ROUND, QMAX, ALU.add, ALU.min))
                    vlink(dve, dve.tensor_scalar(z, z, -QMAX, y_max[:, 2:3], ALU.max, ALU.mult))
                    vlink(dve, dve.tensor_tensor(z, z, y, ALU.subtract))
                    vlink(dve, dve.tensor_tensor(z, y, z, ALU.add))
                    vlink(dve, dve.tensor_tensor(x[:, t, :], x[:, t, :], z, ALU.add))
                    last = stat(1, t)
                vlink(dve, last)

            def experts():
                dve.wait_ge(m["lg"], 1)
                dve.wait_ge(m["w"], 16)
                lg = ps[:, 4, 0:NT * E_].rearrange("p (t e) -> p t e", e=E_)

                def wide(v):
                    return v.unsqueeze(2).broadcast_to([P, NT, E_])

                dve.memset(onehot_pad[:, 0:before], 0.0)
                vlink(dve, dve.tensor_reduce(g_max[:, :], lg, AX.X, ALU.max))
                dve.tensor_tensor(gm[:, :, :], lg, wide(g_max[:, :]), ALU.subtract).then_inc(m["ex_in"], 1)
                dve.wait_ge(m["ex"], 1)
                vlink(dve, dve.tensor_reduce(g_sum[:, :], gl[:, :, :], AX.X, ALU.add))
                vlink(dve, dve.reciprocal(g_rec[:, :], g_sum[:, :]))
                vlink(dve, dve.tensor_tensor(gl[:, :, :], gl[:, :, :], wide(g_rec[:, :]), ALU.mult))
                vlink(dve, dve.tensor_reduce(g_max[:, :], gl[:, :, :], AX.X, ALU.max))
                vlink(dve, dve.tensor_tensor(gt[:, :, :], gl[:, :, :], wide(g_max[:, :]), ALU.is_equal))
                vlink(dve, dve.tensor_tensor(gt[:, :, :], gt[:, :, :], rev8[:, :, :], ALU.mult))
                vlink(dve, dve.tensor_reduce(g_first[:, :], gt[:, :, :], AX.X, ALU.max))
                vlink(dve, dve.tensor_tensor(onehot[:, :, :], rev8[:, :, :], wide(g_first[:, :]), ALU.is_equal))
                dve.tensor_copy(onehot_b[:, :, :], onehot[:, :, :]).then_inc(m["oh"], 1)
                dve.wait_ge(m["cum"], 1)
                cum = ps[:, 5, 0:NT * E_].rearrange("p (t e) -> p t e", e=E_)
                vlink(dve, dve.scalar_tensor_tensor(gt[:, :, :], cum, -1.0, onehot[:, :, :], ALU.add, ALU.mult))
                vlink(dve, dve.tensor_reduce(g_pos[:, :], gt[:, :, :], AX.X, ALU.add))
                vlink(dve, dve.tensor_scalar(g_keep[:, :], g_pos[:, :], float(C_), None, ALU.is_lt))
                dve.tensor_tensor(g_val[:, :], g_max[:, :], g_keep[:, :], ALU.mult)
                vlink(dve, dve.tensor_scalar(g_off[:, :], g_first[:, :], -float(C_), float(E_ * C_), ALU.mult, ALU.add))
                vlink(dve, dve.tensor_tensor(g_slot[:, :], g_off[:, :], g_pos[:, :], ALU.add))
                vlink(dve, dve.tensor_scalar(g_keep[:, :], g_keep[:, :], -float(4 * N), float(4 * N), ALU.mult, ALU.add))
                vlink(dve, dve.tensor_tensor(g_slot[:, :], g_slot[:, :], g_keep[:, :], ALU.add))
                dve.tensor_copy(slot_put[:, :], g_slot[:, :])
                vlink(dve, dve.tensor_scalar(g_pos[:, :], g_pos[:, :], float(C_ - 1), None, ALU.min))
                vlink(dve, dve.tensor_tensor(g_slot[:, :], g_off[:, :], g_pos[:, :], ALU.add))
                dve.tensor_copy(slot_get[:, :], g_slot[:, :]).then_inc(m["slots"], 1)
                dve.wait_ge(m["b2"], 32)

                def take(e):
                    dve.wait_ge(m["tp"], e + 1)
                    if e >= 2:
                        dve.wait_ge(m["h"], (e - 1) * (F_ // P))
                    dve.tensor_copy(disp_t[e % 2][:, :, :], ps[:, 0, :].rearrange("p (k n) -> p k n", k=KD))\
                       .then_inc(m["dt"], 1)

                take(0)
                for e in range(E_):
                    if e + 1 < E_:
                        take(e + 1)
                    for c in range(2):
                        v = 2 * e + c
                        dve.wait_ge(m["y"], v + 1)
                        if e >= 2 and c == 0:
                            dve.wait_ge(m[f"st{e % 2}"], 16 * (e // 2))
                        dve.tensor_tensor(eo[e % 2][:, c, :], ps[:, 6 + v % 2, 0:D], b2_all[:, e, :], ALU.add)\
                           .then_inc(m["yev"], 1)
                dve.wait_ge(m["get"], 16 * NT)
                for t in range(NT):
                    dve.scalar_tensor_tensor(x[:, t, :], back[:, t, :], g_val[:, t:t + 1], x[:, t, :],
                                             ALU.mult, ALU.add).then_inc(m["xadd"], 1)
                for t in range(NT):
                    dve.wait_ge(m["xadd"], t + 1)
                    last = stat(3, t)
                vlink(dve, last)

            def leaves():
                dve.wait_ge(f["w"], 16 * 6)
                dve.memset(sel[:, :, :], 0.0)
                for i in range(3):
                    dve.wait_ge(f["leafc"], 16 * (i + 1))
                    dve.tensor_copy(leaf_b[i][0:96, :], leaf_f[0:96, :]).then_inc(f["ndev"], 1)
                dve.wait_ge(f["nd"], 1)
                for a in range(2):
                    vlink(dve, dve.tensor_tensor(
                        go[:, 8 * a:8 * a + 8, :], ps[:, 2 + a, 0:384].rearrange("p (t n) -> p t n", n=48),
                        node_b.unsqueeze(1).broadcast_to([P, 8, 48]), ALU.add))
                vlink(dve, dve.tensor_scalar(go[:, :, :], go[:, :, :], 0.0, None, ALU.is_ge))
                g3 = go.rearrange("p t (i n) -> p (t i) n", n=16)
                vlink(dve, dve.tensor_copy(path[0][:, :, 1:2], g3[:, :, 0:1]))
                vlink(dve, dve.tensor_scalar(path[0][:, :, 0:1], g3[:, :, 0:1], -1.0, 1.0, ALU.mult, ALU.add))
                for lv in range(1, 4):
                    w = 1 << lv
                    par = path[lv - 1][:, :, :]
                    if lv < 3:
                        ch = path[lv].rearrange("p a (n c) -> p a n c", c=2)
                    else:
                        ch = sel.rearrange("p t (i n) -> p (t i) n", n=32)[:, :, 0:16]\
                                .rearrange("p a (n c) -> p a n c", c=2)
                    vlink(dve, dve.tensor_tensor(ch[:, :, :, 1], par, g3[:, :, w - 1:2 * w - 1], ALU.mult))
                    last = dve.tensor_tensor(ch[:, :, :, 0], par, ch[:, :, :, 1], ALU.subtract)
                    if lv < 3:
                        vlink(dve, last)
                last.then_inc(f["sel"], 1)
                for u in range(NT // 4):
                    dve.wait_ge(f["selt"], u + 1)
                    dve.tensor_scalar(nsel_t[0:96, u * CH:(u + 1) * CH], ps[0:96, 4 + u % 2, :], -1.0, 1.0,
                                      ALU.mult, ALU.add).then_inc(f["nselt"], 1)
                yu = 0
                for i in range(3):
                    for c in range(NCH):
                        if i < 2:
                            for k in range(KD):
                                dve.wait_ge(f["y"], yu + 1)
                                dve.tensor_copy((fq_t, fk_t)[i][:, k, c * CH:(c + 1) * CH], ps[:, yu % 2, :])\
                                   .then_inc(f["yev"], 1)
                                yu += 1
                        else:
                            for t in range(4):
                                dve.wait_ge(f["y"], yu + 1)
                                dve.tensor_copy(fv[:, 4 * c + t, :], ps[:, yu % 2, 0:D]).then_inc(f["yev"], 1)
                                yu += 1

                def maxima(t):
                    dve.wait_ge(f["sc"], t + 1)
                    vlink(dve, dve.tensor_reduce(f_mx[:, t:t + 1], ps[:, 2 * (t % 2):2 * (t % 2) + 2, :]
                                                 .rearrange("p a n -> p (a n)"), AX.X, ALU.max))
                    dve.tensor_scalar(f_nmx[:, t:t + 1], f_mx[:, t:t + 1], -(D ** -0.5), None, ALU.mult)\
                       .then_inc(f["mx"], 1)

                dve.wait_ge(s_xback, 16 * B + 16)
                maxima(0)
                for t in range(NT):
                    if t + 1 < NT:
                        maxima(t + 1)
                    dve.wait_ge(f["ptp"], t + 1)
                    if t >= 2:
                        dve.wait_ge(f["o"], t - 1)
                    dve.tensor_copy(f_pt[t % 2][:, 4:8, :], ps[:, 5, :].rearrange("p (k n) -> p k n", n=P))\
                       .then_inc(f["ptev_v"], 1)
                    if t:
                        weigh(t - 1)
                weigh(NT - 1)

            def weigh(t):
                dve.wait_ge(f["o"], t + 1)
                vlink(dve, dve.reciprocal(f_rec[:, t:t + 1], f_sum[:, t:t + 1]))
                dve.scalar_tensor_tensor(x[:, t, :], ps[:, 6 + t % 2, 0:D], f_rec[:, t:t + 1], x[:, t, :],
                                         ALU.mult, ALU.add).then_inc(f["oev"], 1)

            dve.wait_ge(s_const, 16 * 5)
            dve.tensor_copy(tri_b[:, :], tri_f[:, :])
            dve.tensor_copy(ones_b[:, :], ones[:, :]).then_inc(s_castc, 1)
            dve.wait_ge(s_x, 16)
            for t in range(NT):
                last = stat(0, t)
            vlink(dve, last)
            for n in range(upto):
                layer_norm(n)
                if n in AT:
                    a, s, o, _, _ = AT[n]
                    attention(a, s, o)
                elif n == 2:
                    experts()
                else:
                    leaves()
            dve.memset(tmp_r[:, 0:1], 0.0).then_inc(s_out, 1)

        @block.gpsimd
        def _(pool):
            for n in range(upto):
                if n in AT:
                    a, s, o, _, _ = AT[n]
                    if n == 3:
                        pool.wait_ge(m["xadd"], NT)
                    if n in (0, 3):
                        pool.memset(va[:, :, :], 1.0).then_inc(s_pool0, 1)
                        for i in range(3):
                            pool.wait_ge(s_pool0, 4 * (n // 3) + i + 1)
                            pool.memset(k_stack[i][STACK:STACK + 3, :, :], 1.0).then_inc(s_pool0, 1)
                    for gi in range(B * G):
                        pool.wait_ge(s["rows"], o["rows"] + gi + 1)
                        for r in range(3):
                            pool.dma_start(q_stack[gi % 3][STACK + r:STACK + r + 1, :, :]
                                           .rearrange("p j (q n) -> p (j q) n", n=P),
                                           row_parts[0:32, gi % 2, r, :]).then_inc(s[f"rl{gi % 3}"], 16)
                    if a.quant:
                        pool.wait_ge(s["ymax"], o["ymax"] + 1)
                        pool.partition_all_reduce(y_max[:, 1:2], y_max[:, 0:1], P, bass.bass_isa.ReduceOp.max)\
                            .then_inc(s["ygmax"], 1)
                elif n == 2:
                    pool.wait_ge(s_ln["ln_xn"][n], 1)
                    scalar_done(pool, n - 1)
                    pool.memset(zero[:, :, :], 0.0).then_inc(m["zero"], 1)
                    pool.wait_ge(m["zero"], 1)
                    pool.dma_start(disp_d.rearrange("(p r) n -> p (r n)", p=P),
                                   zero.rearrange("p t n -> p (t n)")).then_inc(m["zeroed"], 16)
                    pool.wait_ge(m["zeroed"], 16)
                    pool.wait_ge(m["slots"], 1)
                    for t in range(NT):
                        pool.indirect_dma_start(
                            disp_d, bass.IndirectOffsetOnAxis(ap=slot_put[:, t:t + 1], axis=0), xn[:, t, :], None,
                            bounds_check=N - 1, oob_is_err=False).then_inc(m["put"], 16)
                    pool.wait_ge(m["st0"], 16 * E_ // 2)
                    pool.wait_ge(m["st1"], 16 * E_ // 2)
                    for t in range(NT):
                        pool.indirect_dma_start(
                            back[:, t, :], None, eo_d, bass.IndirectOffsetOnAxis(ap=slot_get[:, t:t + 1], axis=0),
                            bounds_check=N - 1, oob_is_err=False).then_inc(m["get"], 16)

        @block.sync
        def _(sp):
            sp.dma_start(x[:, :, :], d["x"].rearrange("(t p) n -> p t n", p=P)).then_inc(s_x, 16)
            for t_, n_ in ((ident, "c_ident"), (rot, "c_rot"), (ones, "c_ones"), (tri_f, "c_tri")):
                sp.dma_start(t_[:, :], d[n_]).then_inc(s_const, 16)
            sp.dma_start(rev8_c[:, :], d["c_rev8"]).then_inc(s_const, 16)
            for n in range(upto):
                if n in AT:
                    a, s, o, qp, kp = AT[n]
                    if n:
                        sp.wait_ge(s_ln["ln_xn"][n], 1)
                        scalar_done(sp, n - 1)
                    w = d[a.name]
                    for c in "qkvo":
                        sp.dma_start(w_of[c][:, :, :], w["w" + c].rearrange("(k p) n -> p k n", p=P))\
                          .then_inc(s["w"], 16)
                    if a.bias:
                        sp.dma_start(bq, w["bq"]).then_inc(s["w"], 16)
                        sp.dma_start(bk, w["bk"]).then_inc(s["w"], 16)
                        sp.dma_start(bv, w["bv"].unsqueeze(0).broadcast_to([P, D])).then_inc(s["w"], 16)
                        sp.dma_start(bo, w["bo"].unsqueeze(0).broadcast_to([P, D])).then_inc(s["w"], 16)
                    if a.cross:
                        sp.dma_start(ctx_t[:, :, :], d["ctx_t"].rearrange("(k p) n -> p k n", p=P))\
                          .then_inc(s["w"], 16)
                    if a.rope:
                        sp.dma_start(cos_t, d["c_cos"]).then_inc(s["w"], 16)
                        sp.dma_start(sin_t, d["c_sin"]).then_inc(s["w"], 16)

                    if a.mixed:
                        sp.wait_ge(s_ln["ln_xn"][n], NT)
                        sp.dma_start(x_d.rearrange("(t p) n -> p t n", p=P), x[:, :, :]).then_inc(s_xmix, 16)

                    us = units(a)
                    stored = [0]

                    def store(u):
                        which, b, hh, c, w_ = us[u]
                        sp.wait_ge(s["split"], o["split"] + u + 1)
                        dst = (qp if which == "q" else kp)[:, hh * P:(hh + 1) * P, c:c + w_]
                        sp.dma_start(dst.rearrange("s p n -> p s n"), parts[u % 2][:, :, 0:w_])\
                          .then_inc(s[f"st{u % 2}"], 16)
                        stored[0] = u + 1

                    def load(gi):
                        b, g = divmod(gi, G)
                        sp.wait_ge(s["st0"], o["st0"] + 16 * ((stored[0] + 1) // 2))
                        sp.wait_ge(s["st1"], o["st1"] + 16 * (stored[0] // 2))
                        if gi >= 3:
                            sp.wait_ge(s["ex"], o["ex"] + 2 * a.steps * (gi - 2))
                        nk = a.keys
                        for blk in range(6):
                            rows = slice(16 * blk, 16 * blk + 16)
                            sp.dma_start(q_stack[gi % 3][rows, :, :],
                                         qp[QPART[blk], 64 * g:64 * g + 64, b * S:(b + 1) * S]
                                         .rearrange("(j r) n -> r j n", r=DH)).then_inc(s[f"ldk{gi % 3}"], 16)
                            sp.dma_start(k_stack[gi % 3][rows, :, 0:nk],
                                         kp[KPART[blk], 64 * g:64 * g + 64, b * nk:(b + 1) * nk]
                                         .rearrange("(j r) n -> r j n", r=DH)).then_inc(s[f"ldk{gi % 3}"], 16)

                    pair = {gi: max(u for u in range(len(us)) if us[u][0] == "q" and us[u][1:3] == (0, gi // 2)) + 1
                            + (0 if a.cross else 2) for gi in range(3)}
                    gi = 0
                    for u in range(len(us)):
                        store(u)
                        while gi < 3 and pair[gi] == u + 1:
                            load(gi)
                            gi += 1
                    if a.mixed:
                        sp.wait_ge(s_xmix, 16)
                        for b in range(B):
                            sp.dma_start(x[64 * b:64 * b + 64, :, :],
                                         x_d[b * S:(b + 1) * S, :].rearrange("(t r) n -> r t n", r=64))\
                              .then_inc(s_xmix, 16)
                    for gi in range(3, B * G):
                        load(gi)
                elif n == 2:
                    sp.wait_ge(s_ln["ln_xn"][n], 1)
                    scalar_done(sp, n - 1)
                    w = d["moe"]
                    sp.dma_start(wg[:, :, :], w["wg"].rearrange("(k p) n -> p k n", p=P)).then_inc(m["w"], 16)
                    sp.dma_start(ff_bias, w["b1"]).then_inc(m["b2"], 16)
                    sp.wait_ge(m["b2"], 16)
                    sp.dma_start(b2_all.rearrange("p e n -> p (e n)"),
                                 w["b2"].rearrange("(a e) n -> a (e n)", a=1).broadcast_to([P, E_ * D]))\
                      .then_inc(m["b2"], 16)

                    def weights(e):
                        if e >= 3:
                            sp.wait_ge(m["y"], 2 * (e - 2))
                        sp.dma_start(w1e[e % 3][:, :, :], w["w1"][e].rearrange("(k p) n -> p k n", p=P))\
                          .then_inc(m[f"w1_{e % 3}"], 16)
                        sp.dma_start(w2e[e % 3][:, :, :], w["w2"][e].rearrange("(k p) n -> p k n", p=P))\
                          .then_inc(m[f"w1_{e % 3}"], 16)

                    def tokens(e):
                        if e >= 2:
                            sp.wait_ge(m["tp"], e - 1)
                        sp.dma_start(disp[e % 2][:, :, :],
                                     disp_d[e * C_:(e + 1) * C_, :].rearrange("(c p) n -> p c n", p=P))\
                          .then_inc(m[f"dl{e % 2}"], 16)

                    for e in range(3):
                        weights(e)
                    sp.wait_ge(m["put"], 16 * NT)
                    tokens(0)
                    tokens(1)
                    for e in range(E_):
                        if e + 2 < E_:
                            tokens(e + 2)
                        sp.wait_ge(m["yev"], 2 * e + 2)
                        sp.dma_start(eo_d[e * C_:(e + 1) * C_, :].rearrange("(c p) n -> p c n", p=P), eo[e % 2][:, :, :])\
                          .then_inc(m[f"st{e % 2}"], 16)
                        if e + 3 < E_:
                            weights(e + 3)
                else:
                    sp.wait_ge(s_ln["ln_xn"][n], 1)
                    scalar_done(sp, n - 1)
                    w = d["fff"]
                    sp.dma_start(nodes[:, :, :], w["nodes"].rearrange("(k p) n -> p k n", p=P)).then_inc(f["w"], 16)
                    sp.dma_start(node_b, w["node_b"].unsqueeze(0).broadcast_to([P, 48])).then_inc(f["w"], 16)
                    sp.dma_start(fb2[0:96, :, :], w["b2"]).then_inc(f["w"], 16)
                    for i in range(3):
                        sp.dma_start(fb1[:, i, :], w[f"b1{i}"]).then_inc(f["w"], 16)
                    for i in range(3):
                        if i:
                            sp.wait_ge(f["ndev"], i)
                        sp.dma_start(leaf_f[0:96, :], d["c_leaf"][i]).then_inc(f["leafc"], 16)
                    sp.wait_ge(s_ln["ln_xn"][n], NT)
                    for b in range(B):
                        sp.dma_start(x_mixed_d[b * S:(b + 1) * S, :].rearrange("(t r) n -> r t n", r=64),
                                     x[64 * b:64 * b + 64, :, :]).then_inc(s_xback, 16)
                    for i in range(3):
                        if i == 2:
                            sp.wait_ge(s_xback, 16 * B)
                            sp.dma_start(x[:, :, :], x_mixed_d.rearrange("(t p) n -> p t n", p=P))\
                              .then_inc(s_xback, 16)
                            sp.wait_ge(f["y"], 2 * NCH)
                        sp.dma_start(fw1[i % 2][:, :, :], w[f"w1{i}"].rearrange("(k p) n -> p k n", p=P))\
                          .then_inc(f[f"wl{i % 2}"], 16)
                        sp.dma_start(fw2[i % 2][:, :, :], w[f"w2{i}"].rearrange("(k p) n -> p k n", p=P))\
                          .then_inc(f[f"wl{i % 2}"], 16)
            sp.wait_ge(s_out, 1)
            sp.dma_start(out.rearrange("(t p) n -> p t n", p=P), x[:, :, :]).then_inc(s_out, 16)
            sp.wait_ge(s_out, 17)


def _constants():
    import numpy as np

    c = {"c_ident": np.eye(P, dtype=np.float32), "c_ones": np.ones((P, P), np.float32)}
    c["c_tri"] = np.triu(np.ones((P, P), np.float32))
    c["c_rev8"] = np.tile((E_ - np.arange(E_)).astype(np.float32), (P, NT))
    rot = np.zeros((P, P), np.float32)
    for h in range(P // DH):
        for i in range(DH // 2):
            rot[h * DH + 2 * i + 1, h * DH + i] = -1.0
            rot[h * DH + 2 * i, h * DH + DH // 2 + i] = 1.0
    c["c_rot"] = rot
    inv = np.float32(1.0) / np.power(np.float32(10000.0), np.arange(0, DH, 2, dtype=np.float32) / np.float32(DH))
    fr = np.arange(S, dtype=np.float32)[:, None] * inv[None, :]
    emb = np.concatenate([fr, fr], axis=-1)
    c["c_cos"] = np.ascontiguousarray(np.tile(np.cos(emb).astype(np.float32).T, (P // DH, 1)))
    c["c_sin"] = np.ascontiguousarray(np.tile(np.sin(emb).astype(np.float32).T, (P // DH, 1)))
    leaf = np.zeros((3, 96, F_), np.float32)
    for i in range(3):
        for n in range(NLEAF):
            leaf[i, 32 * i + n, n * LEAFW:(n + 1) * LEAFW] = NEG
    c["c_leaf"] = leaf
    return c


def kernel(**inputs):
    import numpy as np
    import concourse.bacc as bacc
    from concourse.bass_utils import run_bass_kernel_spmd as run

    a = {k: np.asarray(v) for k, v in inputs.items()}
    arrays = dict(_constants())
    arrays["x"] = a["x"].reshape(N, D)
    arrays["ctx_t"] = a["ctx_1024"].reshape(B * L, D).T
    names = {"self0": ("L0_attn_W", "L0_attn_b", "qkvo"), "cross0": ("L0_xattn_w", "L0_xattn_b", "qkvo"),
             "self1": ("L1_attn_W", None, "qkvo"), "cross1": ("L1_xattn_W", "L1_xattn_b", "qkvh")}
    for st, (w, b, cs) in names.items():
        for c, to in zip(cs, "qkvo"):
            arrays[f"{st}.w{to}"] = a[w + c].T
            if b:
                arrays[f"{st}.b{to}"] = a[b + c].reshape(KD, P).T if to in "qk" else a[b + c]
    for n in ("wg", "w1", "b1", "w2", "b2"):
        arrays["moe." + n] = a["L0_ffn_" + n]
    arrays["moe.b1"] = arrays["moe.b1"].reshape(E_ * F_ // P, P).T
    nodes, node_b = np.zeros((D, 48), np.float32), np.zeros(48, np.float32)
    b2 = np.zeros((96, 3, D), np.float32)
    for i, c in enumerate("qkv"):
        p = f"L1_ffn_{c}_"
        nodes[:, 16 * i:16 * i + NNODE] = a[p + "node_w"].T
        node_b[16 * i:16 * i + NNODE] = a[p + "node_b"]
        b2[32 * i:32 * i + NLEAF, i, :] = a[p + "b2"]
        arrays[f"fff.w1{i}"] = a[p + "w1"].transpose(1, 0, 2).reshape(D, F_)
        arrays[f"fff.w2{i}"] = a[p + "w2"].reshape(F_, D)
        arrays[f"fff.b1{i}"] = a[p + "b1"].reshape(F_ // P, P).T
    arrays["fff.nodes"], arrays["fff.node_b"], arrays["fff.b2"] = nodes, node_b, b2
    arrays = {k: np.ascontiguousarray(v) for k, v in arrays.items()}

    nc = bacc.Bacc("TRN2", target_bir_lowering=False, num_devices=1)
    d, feed = {}, {}
    for k, v in arrays.items():
        name = "in_" + k.replace(".", "_")
        feed[name] = v
        ap = nc.dram_tensor(name, v.shape, mybir.dt.from_np(v.dtype), kind="ExternalInput").ap()
        if "." in k:
            st, w = k.split(".")
            d.setdefault(st, {})[w] = ap
        else:
            d[k] = ap
    out = nc.dram_tensor("out", (N, D), F32, kind="ExternalOutput").ap()
    decoder_kernel(nc, d, out)
    r = run(nc, [feed], core_ids=[0])
    return r.results[0]["out"].reshape(B, S, D)
```

```python
from contextlib import ExitStack

import concourse.bass as bass
from concourse import mybir

F32 = mybir.dt.float32
BF16 = mybir.dt.bfloat16
U32 = mybir.dt.uint32
ALU = mybir.AluOpType
ACT = mybir.ActivationFunctionType
AX = mybir.AxisListType

P = 128
B, S, D = 2, 1024, 256
N = B * S
NT = N // P
KD = D // P
H, DH = 16, 16
G = H // 4
L = 77
CH = 512
NCH = N // CH
EPS = 1e-5
E_, C_, F_ = 8, N // 8, 1024
NLEAF, LEAFW, NNODE = 16, 64, 15
VW = DH + 1
VROW = H * VW + 15
STACK = 96
QPART = (0, 0, 1, 1, 0, 2)
KPART = (0, 1, 0, 1, 2, 0)
NEG = -1e30
ROUND = 12582912.0
QMAX = 7.0
THRESH = 0.05
SUBLAYERS = 6


PARTS = 4


class Stage:

    def __init__(self, name, keys, ternary=False, rope=False, quant=False, bias=True, mixed=False, index=0):
        self.name, self.keys, self.ternary, self.rope = name, keys, ternary, rope
        self.quant, self.bias, self.index = quant, bias, index
        self.mixed = mixed
        self.cross = keys == L
        self.ktiles = 1 if self.cross else keys // P
        self.krows = L if self.cross else P
        self.steps = self.ktiles * (S // CH)
        self.ring = 5 if self.cross else 3
        self.early, self.fill = (6, 3) if self.cross else (8, 3)
        self.kch = 1 if self.cross else keys // CH
        items, late = [], []
        for gi in range(B * G):
            n = 0
            for qt in range(S // P):
                for j in range(1 if self.cross else 4):
                    for kc in range(self.kch):
                        items.append(("m", gi, qt, j, kc))
                        n += 1
                        if n == 3 and late:
                            items.append(late.pop())
            late.append(("t", gi))
        items.append(late.pop())
        self.items = items
        self.per_group = (S // P) * (1 if self.cross else 4) * self.kch
        self.t_at = {it[1]: n for n, it in enumerate(items) if it[0] == "t"}
        self.m_end = {}
        for n, it in enumerate(items):
            if it[0] == "m":
                self.m_end[it[1]] = n
        self.m_before = []
        c = 0
        for it in items:
            self.m_before.append(c)
            c += it[0] == "m"

    def lead(self, step, quarter=4):
        per = self.per_group + 1
        first = 3 * per - 1 if self.cross else per + 17
        return min(len(self.items), first + ((4 * step + quarter) * per) // (4 * self.steps))


SELF0 = Stage("self0", S, ternary=True, quant=True, index=0)
CROSS0 = Stage("cross0", L, index=1)
SELF1 = Stage("self1", S, rope=True, bias=False, index=3)
CROSS1 = Stage("cross1", L, mixed=True, index=4)
ATTN = (SELF0, CROSS0, SELF1, CROSS1)


def units(a):
    out = [("k", 0, hh, 0, B * L) for hh in range(KD)] if a.cross else []
    for b in range(B):
        for hh in range(KD):
            for which in "q" if a.cross else "qk":
                out += [(which, b, hh, b * S + c, CH) for c in range(0, S, CH)]
    return out


def pool_marks(a):
    return 4 if a.index < 2 else 8


def weight_loads(a):
    return 4 + 4 * a.bias + a.cross


def step_counts(a):
    nu, tiles, steps, groups = len(units(a)), B if a.cross else NT, B * G * a.steps, B * G
    c = {
        "pj": nu, "pj_act": nu, "split": nu, "hi": nu, "pj_cos": nu * a.rope,
        "pj_rot": nu * a.rope, "pj_roped": nu * a.rope, 
        "vpj": tiles, "vev": tiles, "sc": 2 * steps, "ex": 2 * steps, "pv": steps, "oev": B * G * (S // CH),
        "mi": len(a.items), "mfree": len(a.items), "mxr": 0 if a.cross else groups, "rows": groups,
        "tern_sum": 2 * a.ternary, "tern_tot": 2 * a.ternary, "wready": 1 * a.ternary,
        "ymax": 1 * a.quant, "ygmax": 1 * a.quant,
    }
    for i in range(PARTS):
        c[f"st{i}"] = 16 * len(range(i, nu, PARTS))
    for i in range(5):
        used = len(range(i, groups, a.ring)) if i < a.ring else 0
        c[f"ldq{i}"], c[f"rl{i}"] = 16 * 6 * used, 16 * 3 * used
        c[f"ldk{i}"] = 16 * 6 * (i == 0) if a.cross else 16 * 6 * used
    for n in ("otp", "ocx", "ctp", "cev", "yp", "yev"):
        c[n] = NT
    return c


def decoder_kernel(nc, d, out):
    ctx = ExitStack()
    with ctx:
        def sb(name, shape, dt=F32):
            return ctx.enter_context(nc.sbuf_tensor(name, shape, dt))

        def sem(name):
            return ctx.enter_context(nc.semaphore(name))

        x = sb("x", [P, NT, D])
        norm = sb("norm", [P, 2 * NT * D])
        xn = norm[:, 0:NT * D].rearrange("p (t n) -> p t n", t=NT)
        xn_t = norm[:, NT * D:].rearrange("p (k n) -> p k n", k=KD)
        o_t = norm[:, :].rearrange("p (g n) -> p g n", g=G)
        ident = sb("ident", [P, P])
        rot = sb("rot", [P, P])
        ones = sb("ones", [P, P])
        ones_b = sb("ones_b", [P, P], BF16)
        tri_b = sb("tri_b", [P, P], BF16)
        stats = sb("stats", [P, NT, 6])
        mv = sb("mv", [P, NT, 2])
        ve = sb("ve", [P, NT])
        sd = sb("sd", [P, NT])
        rstd = sb("rstd", [P, NT])
        tmp_r = sb("tmp_r", [P, NT])
        y_max = sb("y_max", [P, 4])
        tri_f = sb("tri_f", [P, P])
        rev8_c = sb("rev8_c", [P, NT * E_])
        rev8 = rev8_c[:, :].rearrange("p (t e) -> p t e", t=NT)
        wg = sb("wg", [P, KD, E_])
        nodes = sb("nodes", [P, KD, 48])
        node_b = sb("node_b", [P, 48])
        AW = 36864
        arena = sb("arena", [P, AW])
        top = [0]

        def cut(words, dt=F32):
            a = arena[:, top[0]:top[0] + words]
            top[0] += words
            assert top[0] <= AW, top[0]
            return a if dt == F32 else a.bitcast(dt)

        def weight_set(take):
            sets = {c: take(KD * D).rearrange("p (k n) -> p k n", k=KD) for c in "qkvo"}
            sets.update(bq=take(KD), bk=take(KD), bv=take(D), bo=take(D))
            return sets

        own_w = sb("own_w", [P, 4 * KD * D + 2 * KD + 2 * D + KD * B * L])
        top[0] = AW - (4 * KD * D + 2 * KD + 2 * D)
        high_w = weight_set(cut)
        own_top = [0]

        def own(words):
            own_top[0] += words
            return own_w[:, own_top[0] - words:own_top[0]]

        low_w = weight_set(own)
        ctx_t = own(KD * B * L).rearrange("p (k n) -> p k n", k=KD)
        weights_of = {0: high_w, 1: low_w, 3: high_w, 4: low_w}
        top[0] = 0
        q_stack = [cut(4 * S // 2, BF16).rearrange("p (j n) -> p j n", j=4) for _ in range(3)]
        k_stack = [cut(4 * S // 2, BF16).rearrange("p (j n) -> p j n", j=4) for _ in range(3)]
        va = cut(NT * VROW).rearrange("p (t n) -> p t n", t=NT)
        probs = [cut(4 * CH).rearrange("p (j n) -> p j n", j=4) for _ in range(2)]
        proj = [cut(CH) for _ in range(2)]
        rest = [cut(CH) for _ in range(2)]
        roped = [cut(CH) for _ in range(2)]
        parts = [cut(3 * CH // 2, BF16).rearrange("p (s n) -> p s n", s=3) for _ in range(PARTS)]
        mx_raw = cut(2 * 32).rearrange("p (k n) -> p k n", k=2)
        mx = cut(2 * 32).rearrange("p (k n) -> p k n", k=2)
        row_rest = cut(P)
        row_parts = cut(2 * 3 * P // 2, BF16).rearrange("p (a s n) -> p a s n", a=2, s=3)
        rec = [cut(H) for _ in range(2)]
        ctxn = [cut(D) for _ in range(2)]
        ctxn_t = [cut(D).rearrange("p (k n) -> p k n", k=KD) for _ in range(2)]
        ahead = top[0]
        cos_t = cut(S)
        sin_t = cut(S)
        keys_flat = k_stack[0].rearrange("p j n -> p (j n)")
        keys_all = keys_flat[:, 0:H * B * L].rearrange("p (h n) -> p h n", h=H)
        q_ring = q_stack + k_stack[1:]
        top[0] = 0
        y_all = cut(NT * D).rearrange("p (t n) -> p t n", t=NT)
        ctx_rows = y_all
        top[0] = 0
        w_abs = [cut(KD * D) for _ in range(4)]
        w_pos = cut(KD * D)
        w_neg = cut(KD * D)
        tern_s = cut(8)
        tern_d = cut(4)
        tern_n = cut(4)
        tern_a = cut(4)
        tern_c = cut(4)
        top[0] = 0
        ff_bias = cut(E_ * F_ // P)
        b2_all = cut(E_ * D).rearrange("p (e n) -> p e n", e=E_)
        gl = cut(NT * E_).rearrange("p (t e) -> p t e", t=NT)
        gm = cut(NT * E_).rearrange("p (t e) -> p t e", t=NT)
        gt = cut(NT * E_).rearrange("p (t e) -> p t e", t=NT)
        onehot = cut(NT * E_).rearrange("p (t e) -> p t e", t=NT)
        before = (NT - 1) * E_
        onehot_pad = cut((before + NT * E_) // 2, BF16)
        onehot_b = onehot_pad[:, before:].rearrange("p (t e) -> p t e", t=NT)
        g_max = cut(NT)
        g_sum = cut(NT)
        g_rec = cut(NT)
        g_first = cut(NT)
        g_pos = cut(NT)
        g_keep = cut(NT)
        g_val = cut(NT)
        g_off = cut(NT)
        g_slot = cut(NT)
        slot_put = cut(NT, U32)
        slot_get = cut(NT, U32)
        g_back = cut(NT)
        w1e = [cut(KD * F_).rearrange("p (k n) -> p k n", k=KD) for _ in range(2)]
        w2e = [cut((F_ // P) * D).rearrange("p (k n) -> p k n", n=D) for _ in range(2)]
        disp = [cut(2 * D).rearrange("p (s n) -> p s n", s=2) for _ in range(2)]
        disp_t = [cut(KD * C_).rearrange("p (k n) -> p k n", k=KD) for _ in range(2)]
        hid = [cut((F_ // P) * C_).rearrange("p (k n) -> p k n", n=C_) for _ in range(2)]
        eo = [cut(2 * D).rearrange("p (s n) -> p s n", s=2) for _ in range(2)]
        back = cut(NT * D).rearrange("p (t n) -> p t n", t=NT)
        assert top[0] <= ahead
        top[0] = ahead
        w1e.insert(0, cut(KD * F_).rearrange("p (k n) -> p k n", k=KD))
        w2e.insert(0, cut((F_ // P) * D).rearrange("p (k n) -> p k n", n=D))
        go = cut(NT * 48).rearrange("p (t n) -> p t n", t=NT)
        sel_t = cut(N)
        nsel_t = cut(N // 2, BF16)
        top[0] = 0
        path = [cut(NT * 3 * (2 << n)).rearrange("p (a n) -> p a n", n=2 << n) for n in range(3)]
        sel = cut(NT * 96).rearrange("p (t n) -> p t n", t=NT)
        leaf_f = cut(F_)
        leaf_b = [cut(F_ // 2, BF16) for _ in range(3)]
        fb1 = cut(3 * (F_ // P)).rearrange("p (i n) -> p i n", i=3)
        fb2 = cut(3 * D).rearrange("p (i n) -> p i n", i=3)
        fw1 = [w1e[0], cut(KD * F_).rearrange("p (k n) -> p k n", k=KD)]
        fw2 = [w2e[0], cut((F_ // P) * D).rearrange("p (k n) -> p k n", n=D)]
        fh = cut((F_ // P) * CH).rearrange("p (k n) -> p k n", n=CH)
        fq_t = cut(KD * N).rearrange("p (k n) -> p k n", k=KD)
        fk_t = cut(KD * N).rearrange("p (k n) -> p k n", k=KD)
        fv = cut(NT * D).rearrange("p (t n) -> p t n", t=NT)
        f_mx = cut(NT)
        f_nmx = cut(NT)
        f_sum = cut(NT)
        f_rec = cut(NT)
        assert top[0] <= ahead
        f_p = [fw1[0].rearrange("p k n -> p (k n)")[:, 0:S], fw1[0].rearrange("p k n -> p (k n)")[:, S:2 * S]]
        f_pt = [fw2[0].rearrange("p k n -> p (k n)")[:, 0:S].rearrange("p (k n) -> p k n", n=P),
                fw2[0].rearrange("p k n -> p (k n)")[:, S:2 * S].rearrange("p (k n) -> p k n", n=P)]

        ps = ctx.enter_context(nc.psum_tensor("ps", [P, 8, CH], F32))

        def dram(name, shape, dt=F32):
            return nc.dram_tensor(name, shape, dt, kind="Internal").ap()

        q_parts = [dram(f"q_parts{a.index}", [3, D, N], BF16) for a in ATTN]
        k_parts = [dram(f"k_parts{a.index}", [3, D, B * a.keys], BF16) for a in ATTN]
        x_d = dram("x_d", [N, D])
        x_mixed_d = dram("x_mixed_d", [N, D])
        disp_d = dram("disp_d", [N, D])
        eo_d = dram("eo_d", [N, D])

        s_const = sem("s_const")
        s_x = [sem(f"s_x{i}") for i in range(4)]
        s_w = {a.index: sem(f"weights{a.index}") for a in ATTN}
        s_rotary = sem("s_rotary")
        s_castc = sem("s_castc")
        s_xmix = sem("s_xmix")
        s_xback = sem("s_xback")
        s_pool0 = sem("s_pool0")
        ev = sem("dve_order")
        nv = [0]

        def vlink(v, ins):
            nv[0] += 1
            ins.then_inc(ev, 1)
            v.wait_ge(ev, nv[0])

        def per_stage(*names):
            return {n: [sem(f"{n}{i}") for i in range(6)] for n in names}

        s_ln = per_stage("ln_var", "ln_sd", "ln_xn", "ln_tp", "ln_ev")
        s = {n: sem("attn_" + n) for n in step_counts(SELF0)}
        m = {n: sem("moe_" + n) for n in (
            "w", "lg", "ex_in", "ex", "oh", "cum", "slots", "zero", "zeroed", "put", "w1_0", "w1_1", "w1_2", "dl0", "dl1",
            "tp", "dt", "h", "hev", "y", "yev", "b2", "st0", "st1", "xadd")}
        m.update({f"get{i}": sem(f"moe_get{i}") for i in range(4)})
        f = {n: sem("fff_" + n) for n in (
            "w", "nodes", "nd", "ndev", "sel", "tp", "selt", "nselt", "wl0", "wl1", "h", "hev", "y", "yev", "sc", "mx", "ex",
            "ptp", "ptev", "ptev_v", "o", "oev", "leafc")}
        s_out = sem("s_out")

        AT, base = {}, {n: 0 for n in s}
        for a, qp, kp in zip(ATTN, q_parts, k_parts):
            AT[a.index] = (a, s, dict(base), qp, kp)
            base = {n: v + step_counts(a)[n] for n, v in base.items()}

        def keys(a, gi, j, first, count):
            if a.cross:
                b, g = divmod(gi, G)
                at = (4 * g + j) * B * L + b * L + first
                return keys_flat[:, at:at + count]
            return k_stack[gi % a.ring][:, j, first:first + count]

        def scalar_done(eng, n):
            if n in AT:
                eng.wait_ge(s["cev"], AT[n][2]["cev"] + NT)
            elif n == 2:
                eng.wait_ge(m["hev"], E_ * F_ // P)

        block = ctx.enter_context(nc.Block())

        @block.tensor
        def _(pe):
            def layer_norm(n):
                for u in range(NT // 2):
                    pe.wait_ge(s_ln["ln_xn"][n], 2 * u + 2)
                    if u >= 2:
                        pe.wait_ge(s_ln["ln_ev"][n], u - 1)
                    for k in range(KD):
                        for t in range(2):
                            mm = pe.transpose(ps[:, u % 2, (k * 2 + t) * P:(k * 2 + t + 1) * P],
                                              xn[:, 2 * u + t, k * P:(k + 1) * P], ident[:, :])
                    mm.then_inc(s_ln["ln_tp"][n], 1)
                    if n == 2 and u:
                        gate_scores(u - 1)
                    if n == 5 and u:
                        node_scores(u - 1)

            def gate_scores(u):
                pe.wait_ge(s_ln["ln_ev"][2], u + 1)
                if u == 0:
                    pe.wait_ge(m["w"], 16)
                for t in (2 * u, 2 * u + 1):
                    for k in range(KD):
                        mm = pe.matmul(ps[:, 4, t * E_:(t + 1) * E_], xn_t[:, k, t * P:(t + 1) * P], wg[:, k, :],
                                       start=(k == 0), stop=(k == KD - 1))
                if u == NT // 2 - 1:
                    mm.then_inc(m["lg"], 1)

            def node_scores(u):
                pe.wait_ge(s_ln["ln_ev"][5], u + 1)
                if u == 0:
                    pe.wait_ge(f["nodes"], 32)
                for b in range(B):
                    t = b * (NT // 2) + u
                    for k in range(KD):
                        mm = pe.matmul(ps[:, 2 + t // 8, (t % 8) * 48:(t % 8) * 48 + 48],
                                       xn_t[:, k, t * P:(t + 1) * P], nodes[:, k, :],
                                       start=(k == 0), stop=(k == KD - 1))
                if u == NT // 2 - 1:
                    mm.then_inc(f["nd"], 1)

            def attention(a, s, o):
                wts = weights_of[a.index]
                if a.ternary:
                    pe.wait_ge(s["tern_sum"], o["tern_sum"] + 1)
                    pe.matmul(ps[:, 7, 0:4], ones[:, :], tern_s[:, 0:4], start=True, stop=True).then_inc(s["tern_tot"], 1)
                    pe.wait_ge(s["tern_sum"], o["tern_sum"] + 2)
                    pe.matmul(ps[:, 7, 8:16], ones[:, :], tern_s[:, 0:8], start=True, stop=True).then_inc(s["tern_tot"], 1)
                if a.ternary:
                    pe.wait_ge(s["wready"], o["wready"] + 1)
                pe.wait_ge(s_w[a.index], 16 * weight_loads(a))
                pe.wait_ge(s_ln["ln_ev"][a.index], NT // 2)
                done = [0]

                def max_items(limit):
                    while done[0] < min(limit, len(a.items)):
                        n = done[0]
                        it = a.items[n]
                        gi = it[1]
                        if n >= 3:
                            pe.wait_ge(s["mfree"], o["mfree"] + n - 2)
                        bank = 5 + n % 3
                        if it[0] == "t":
                            if a.cross:
                                pe.wait_ge(s["mfree"], o["mfree"] + a.m_end[gi] + 1)
                            else:
                                pe.wait_ge(s["mxr"], o["mxr"] + gi + 1)
                            mm = pe.transpose(ps[0:32, bank, 0:P], mx[:, gi % 2, :], ident[:, :])
                        else:
                            _, _, qt, j, kc = it
                            slot = gi % a.ring
                            if a.m_end.get(gi - 1, -1) < n and (qt, j, kc) == (0, 0, 0):
                                pe.wait_ge(s[f"ldq{slot}"], o[f"ldq{slot}"] + 16 * 6 * (gi // a.ring + 1))
                                kslot, kuse = (0, 1) if a.cross else (slot, gi // a.ring + 1)
                                pe.wait_ge(s[f"ldk{kslot}"], o[f"ldk{kslot}"] + 16 * 6 * kuse)
                            if a.cross:
                                for j in range(4):
                                    mm = pe.matmul(ps[:, bank, j * L:(j + 1) * L],
                                                   q_ring[slot][0:STACK, j, qt * P:(qt + 1) * P],
                                                   keys(a, gi, j, 0, L)[0:STACK], start=True, stop=True)
                            else:
                                mm = pe.matmul(ps[:, bank, :], q_ring[slot][0:STACK, j, qt * P:(qt + 1) * P],
                                               keys(a, gi, j, kc * CH, CH)[0:STACK],
                                               start=True, stop=True)
                        mm.then_inc(s["mi"], 1)
                        done[0] += 1

                for u, (which, b, hh, c, w) in enumerate(units(a)):
                    if u >= 2:
                        pe.wait_ge(s["pj_act"], o["pj_act"] + u - 1)
                    src = xn_t if which == "q" else (ctx_t if a.cross else xn_t)
                    for k in range(KD):
                        mm = pe.matmul(ps[:, u % 2, 0:w], wts[which][:, k, hh * P:(hh + 1) * P],
                                       src[:, k, c:c + w], start=(k == 0), stop=(k == KD - 1))
                    mm.then_inc(s["pj"], 1)
                    if a.rope and u >= 1:
                        rotate(a, s, o, u - 1)
                    if u >= a.early + 2 * a.rope:
                        max_items(done[0] + a.fill)
                if a.rope:
                    rotate(a, s, o, len(units(a)) - 1)
                    max_items(done[0] + a.fill)
                nv_t = B if a.cross else NT
                for t in range(nv_t):
                    if t >= 2:
                        pe.wait_ge(s["vev"], o["vev"] + t - 1)
                    elif t == 0:
                        pe.wait_ge(s["pj_act"], o["pj_act"] + len(units(a)))
                    for k in range(KD):
                        lhs = ctx_t[:, k, t * L:(t + 1) * L] if a.cross else xn_t[:, k, t * P:(t + 1) * P]
                        mm = pe.matmul(ps[0:a.krows, t % 2, 0:D], lhs, wts["v"][:, k, :],
                                       start=(k == 0), stop=(k == KD - 1))
                    mm.then_inc(s["vpj"], 1)
                    max_items(done[0] + a.fill)
                pe.wait_ge(s["vev"], o["vev"] + nv_t)
                pe.wait_ge(s["pj_act"], o["pj_act"] + len(units(a)))
                if a.rope:
                    pe.wait_ge(s["pj_roped"], o["pj_roped"] + len(units(a)))
                pe.wait_ge(s_pool0, pool_marks(a))

                def values(n):
                    gi, r = divmod(n, a.steps)
                    qc, kt = divmod(r, a.ktiles)
                    b, g = divmod(gi, G)
                    pe.wait_ge(s["ex"], o["ex"] + 2 * n + 2)
                    if kt == 0 and n:
                        pe.wait_ge(s["oev"], o["oev"] + n // a.ktiles)
                    for j in range(4):
                        t = b if a.cross else b * (S // P) + kt
                        h = 4 * g + j
                        mm = pe.matmul(ps[32 * j:32 * j + 32, 4, :], va[:, t, h * VW:h * VW + 32],
                                       probs[n % 2][:, j, :], start=(kt == 0), stop=(kt == a.ktiles - 1),
                                       tile_position=(0, 32 * j))
                    mm.then_inc(s["pv"], 1)

                max_items(a.lead(-1))
                total = B * G * a.steps
                for n in range(total):
                    gi, r = divmod(n, a.steps)
                    qc, kt = divmod(r, a.ktiles)
                    if r == 0:
                        slot = gi % a.ring
                        pe.wait_ge(s[f"rl{slot}"], o[f"rl{slot}"] + 16 * 3 * (gi // a.ring + 1))
                    for pr in range(2):
                        e = 2 * n + pr
                        if e >= 2:
                            pe.wait_ge(s["ex"], o["ex"] + e - 1)
                        for j in (2 * pr, 2 * pr + 1):
                            mm = pe.matmul(ps[:, 2 * pr + j % 2, :],
                                           keys(a, gi, j, kt * P, P)[0:STACK + 3],
                                           q_ring[slot][0:STACK + 3, j, qc * CH:(qc + 1) * CH],
                                           start=True, stop=True)
                        mm.then_inc(s["sc"], 1)
                        max_items(a.lead(n, pr + 1))
                    if n:
                        values(n - 1)
                    max_items(a.lead(n))
                values(total - 1)

                def turn(t):
                    if t == 0:
                        pe.wait_ge(s["oev"], o["oev"] + B * G * (S // CH))
                    if t >= 2:
                        pe.wait_ge(s["ocx"], o["ocx"] + t - 1)
                    for i in range(4):
                        if a.mixed:
                            g, place = t // 4, 4 * (t % 4) + i
                            src = o_t[:, g, :].rearrange("p (r m) -> p r m", m=H)[:, :, place]
                        else:
                            src = o_t[:, i, t * P:(t + 1) * P]
                        mm = pe.transpose(ps[:, t % 2, i * P:(i + 1) * P], src, ident[:, :])
                    mm.then_inc(s["otp"], 1)

                def turn_back(t):
                    pe.wait_ge(s["ocx"], o["ocx"] + (4 * (t // 4) + 4 if a.mixed else t + 1))
                    if t >= 2:
                        pe.wait_ge(s["cev"], o["cev"] + t - 1)
                    rows = ctx_rows[:, t, :] if a.mixed else ctxn[t % 2]
                    for k in range(KD):
                        mm = pe.transpose(ps[:, 2 + t % 2, k * P:(k + 1) * P], rows[:, k * P:(k + 1) * P],
                                          ident[:, :])
                    mm.then_inc(s["ctp"], 1)

                def project(t):
                    pe.wait_ge(s["cev"], o["cev"] + t + 1)
                    if t >= 2:
                        pe.wait_ge(s["yev"], o["yev"] + t - 1)
                    elif t == 0:
                        pe.wait_ge(s["mfree"], o["mfree"] + len(a.items))
                    for k in range(KD):
                        mm = pe.matmul(ps[:, 6 + t % 2, 0:D], ctxn_t[t % 2][:, k, :], wts["o"][:, k, :],
                                       start=(k == 0), stop=(k == KD - 1))
                    mm.then_inc(s["yp"], 1)

                lag = 4 if a.mixed else 1
                for t in range(NT + lag + 1):
                    if t < NT:
                        turn(t)
                    if lag <= t < NT + lag:
                        turn_back(t - lag)
                    if t > lag:
                        project(t - lag - 1)

            def rotate(a, s, o, u):
                pe.wait_ge(s["pj_act"], o["pj_act"] + u + 1)
                if u >= 2:
                    pe.wait_ge(s["pj_roped"], o["pj_roped"] + u - 1)
                w = units(a)[u][4]
                pe.matmul(ps[:, 2 + u % 2, 0:w], rot[:, :], proj[u % 2][:, 0:w], start=True, stop=True)\
                  .then_inc(s["pj_rot"], 1)

            def experts():
                n = 2
                pe.wait_ge(s_ln["ln_ev"][n], NT // 2)
                gate_scores(NT // 2 - 1)
                pe.wait_ge(s_castc, 1)
                pe.wait_ge(m["oh"], 1)
                for k in range(NT):
                    mm = pe.matmul(ps[:, 5, 0:NT * E_], (ones_b if k else tri_b)[:, :],
                                   onehot_pad[:, before - k * E_:before - k * E_ + NT * E_],
                                   start=(k == 0), stop=(k == NT - 1))
                mm.then_inc(m["cum"], 1)

                def turn(e):
                    pe.wait_ge(m[f"dl{e % 2}"], 16 * (e // 2 + 1))
                    if e:
                        pe.wait_ge(m["dt"], e)
                    for k in range(KD):
                        for c in range(2):
                            mm = pe.transpose(ps[:, 0, k * C_ + c * P:k * C_ + (c + 1) * P],
                                              disp[e % 2][:, c, k * P:(k + 1) * P], ident[:, :])
                    mm.then_inc(m["tp"], 1)

                turn(0)
                for e in range(E_):
                    pe.wait_ge(m["dt"], e + 1)
                    pe.wait_ge(m[f"w1_{e % 3}"], 32 * (e // 3 + 1))
                    for ht in range(F_ // P):
                        u = e * (F_ // P) + ht
                        if u >= 3:
                            pe.wait_ge(m["hev"], u - 2)
                        for k in range(KD):
                            mm = pe.matmul(ps[:, 1 + u % 3, 0:C_], w1e[e % 3][:, k, ht * P:(ht + 1) * P],
                                           disp_t[e % 2][:, k, :], start=(k == 0), stop=(k == KD - 1))
                        mm.then_inc(m["h"], 1)
                    if e + 1 < E_:
                        turn(e + 1)
                    pe.wait_ge(m["hev"], (e + 1) * (F_ // P))
                    for c in range(2):
                        v = 2 * e + c
                        if v >= 2:
                            pe.wait_ge(m["yev"], v - 1)
                        for ht in range(F_ // P):
                            mm = pe.matmul(ps[:, 6 + v % 2, 0:D], hid[e % 2][:, ht, c * P:(c + 1) * P],
                                           w2e[e % 3][:, ht, :], start=(ht == 0), stop=(ht == F_ // P - 1))
                        mm.then_inc(m["y"], 1)

            def leaves():
                n = 5
                pe.wait_ge(s_ln["ln_ev"][n], NT // 2)
                pe.wait_ge(f["w"], 16 * 4)
                node_scores(NT // 2 - 1)
                pe.wait_ge(f["sel"], 1)
                for u in range(NT // 4):
                    if u >= 2:
                        pe.wait_ge(f["selt"], u - 1)
                        pe.wait_ge(f["nselt"], u - 1)
                    for t in range(4):
                        mm = pe.transpose(ps[0:96, 4 + u % 2, t * P:(t + 1) * P], sel[:, 4 * u + t, :], ident[:, :])
                    mm.then_inc(f["tp"], 1)
                pe.wait_ge(f["selt"], NT // 4)
                pe.wait_ge(f["nselt"], NT // 4)
                pe.wait_ge(f["ndev"], 3)
                hu = yu = 0
                for i in range(3):
                    pe.wait_ge(f[f"wl{i % 2}"], 32 * (i // 2 + 1))
                    for c in range(NCH):
                        for ht in range(F_ // P):
                            if hu >= 3:
                                pe.wait_ge(f["hev"], hu - 2)
                            o = ps[:, 5 + hu % 3, :]
                            for k in range(KD):
                                pe.matmul(o, fw1[i % 2][:, k, ht * P:(ht + 1) * P],
                                          xn_t[:, k, c * CH:(c + 1) * CH], start=(k == 0), stop=False)
                            pe.matmul(o, leaf_b[i][0:96, ht * P:(ht + 1) * P], nsel_t[0:96, c * CH:(c + 1) * CH],
                                      start=False, stop=True).then_inc(f["h"], 1)
                            hu += 1
                        pe.wait_ge(f["hev"], hu)
                        if i < 2:
                            for k in range(KD):
                                if yu >= 2:
                                    pe.wait_ge(f["yev"], yu - 1)
                                o = ps[:, yu % 2, :]
                                for ht in range(F_ // P):
                                    pe.matmul(o, fw2[i % 2][:, ht, k * P:(k + 1) * P], fh[:, ht, :],
                                              start=(ht == 0), stop=False)
                                pe.matmul(o, fb2[0:96, i, k * P:(k + 1) * P], sel_t[0:96, c * CH:(c + 1) * CH],
                                          start=False, stop=True).then_inc(f["y"], 1)
                                yu += 1
                        else:
                            for t in range(4):
                                if yu >= 2:
                                    pe.wait_ge(f["yev"], yu - 1)
                                o = ps[:, yu % 2, 0:D]
                                for ht in range(F_ // P):
                                    pe.matmul(o, fh[:, ht, t * P:(t + 1) * P], fw2[i % 2][:, ht, :],
                                              start=(ht == 0), stop=False)
                                pe.matmul(o, sel_t[0:96, c * CH + t * P:c * CH + (t + 1) * P], fb2[0:96, i, :],
                                          start=False, stop=True).then_inc(f["y"], 1)
                                yu += 1
                pe.wait_ge(f["yev"], yu)

                def scores(t):
                    if t >= 2:
                        pe.wait_ge(f["ex"], t - 1)
                    for kc in range(2):
                        for k in range(KD):
                            mm = pe.matmul(ps[:, 2 * (t % 2) + kc, :], fq_t[:, k, t * P:(t + 1) * P],
                                           fk_t[:, k, (t // 8) * S + kc * CH:(t // 8) * S + (kc + 1) * CH],
                                           start=(k == 0), stop=(k == KD - 1))
                    mm.then_inc(f["sc"], 1)

                def turn(t):
                    pe.wait_ge(f["ex"], t + 1)
                    if t:
                        pe.wait_ge(f["ptev"], t)
                        pe.wait_ge(f["ptev_v"], t)
                    for kt in range(S // P):
                        mm = pe.transpose(ps[:, 4 + kt // 4, (kt % 4) * P:(kt % 4 + 1) * P],
                                          f_p[t % 2][:, kt * P:(kt + 1) * P], ident[:, :])
                    mm.then_inc(f["ptp"], 1)

                def values(t):
                    pe.wait_ge(f["ptev"], t + 1)
                    pe.wait_ge(f["ptev_v"], t + 1)
                    if t >= 2:
                        pe.wait_ge(f["oev"], t - 1)
                    for kt in range(S // P):
                        mm = pe.matmul(ps[:, 6 + t % 2, 0:D], f_pt[t % 2][:, kt, :], fv[:, (t // 8) * 8 + kt, :],
                                       start=(kt == 0), stop=(kt == S // P - 1))
                    mm.then_inc(f["o"], 1)

                scores(0)
                for t in range(NT):
                    if t + 1 < NT:
                        scores(t + 1)
                    turn(t)
                    if t:
                        values(t - 1)
                values(NT - 1)

            pe.wait_ge(s_const, 16 * 5)
            for n in range(SUBLAYERS):
                if n:
                    scalar_done(pe, n - 1)
                layer_norm(n)
                if n in AT:
                    a, s, o, _, _ = AT[n]
                    attention(a, s, o)
                elif n == 2:
                    experts()
                else:
                    leaves()

        @block.scalar
        def _(act):
            def layer_norm(n):
                act.wait_ge(s_ln["ln_var"][n], 1)
                act.activation(sd[:, :], ve[:, :], ACT.Sqrt).then_inc(s_ln["ln_sd"][n], 1)
                for u in range(NT // 2):
                    act.wait_ge(s_ln["ln_tp"][n], u + 1)
                    bank = ps[:, u % 2, :].rearrange("p (k n) -> p k n", k=KD)
                    if n == 5:
                        for k in range(KD):
                            ins = act.activation(
                                xn_t[:, k, :].rearrange("p (b t r) -> p t b r", b=B, r=64)[:, 2 * u:2 * u + 2],
                                bank[:, k, :].rearrange("p (t b r) -> p t b r", t=2, b=B), ACT.Copy)
                        ins.then_inc(s_ln["ln_ev"][n], 1)
                        continue
                    act.activation(xn_t[:, :, 2 * u * P:(2 * u + 2) * P], bank, ACT.Copy)\
                       .then_inc(s_ln["ln_ev"][n], 1)

            def attention(a, s, o):
                if a.ternary:
                    act.wait_ge(s_w[0], 16 * 8)
                    for i, c in enumerate("qkvo"):
                        ins = act.activation(w_abs[i], weights_of[0][c].rearrange("p k n -> p (k n)"), ACT.Abs,
                                             accum_out=tern_s[:, i:i + 1])
                    ins.then_inc(s["tern_sum"], 1)

                def high_part(u):
                    act.wait_ge(s["pj_roped"], o["pj_roped"] + u + 1)
                    if u >= PARTS:
                        i = u % PARTS
                        act.wait_ge(s[f"st{i}"], o[f"st{i}"] + 16 * (u // PARTS))
                    w = units(a)[u][4]
                    act.activation(parts[u % PARTS][:, 0, 0:w], roped[u % 2][:, 0:w], ACT.Copy).then_inc(s["hi"], 1)

                act.wait_ge(s_w[a.index], 16 * weight_loads(a))
                for u, (which, b, hh, c, w) in enumerate(units(a)):
                    act.wait_ge(s["pj"], o["pj"] + u + 1)
                    if u >= 2 and not a.rope:
                        act.wait_ge(s["split"], o["split"] + u - 1)
                    if a.rope:
                        if u >= 2:
                            act.wait_ge(s["pj_roped"], o["pj_roped"] + u - 1)
                        act.activation(proj[u % 2][:, 0:w], ps[:, u % 2, 0:w], ACT.Copy).then_inc(s["pj_act"], 1)
                        if u:
                            high_part(u - 1)
                    else:
                        bias = weights_of[a.index]["b" + which][:, hh:hh + 1]
                        if u >= PARTS:
                            i = u % PARTS
                            act.wait_ge(s[f"st{i}"], o[f"st{i}"] + 16 * (u // PARTS))
                        act.activation(parts[u % PARTS][:, 0, 0:w], ps[:, u % 2, 0:w], ACT.Identity, bias=bias)\
                           .then_inc(s["hi"], 1)
                        act.activation(proj[u % 2][:, 0:w], ps[:, u % 2, 0:w], ACT.Identity, bias=bias)\
                           .then_inc(s["pj_act"], 1)
                if a.rope:
                    high_part(len(units(a)) - 1)
                total = B * G * a.steps
                scale = DH ** -0.5

                def copy_sums(i):
                    gi, qc = divmod(i, S // CH)
                    b, g = divmod(gi, G)
                    act.wait_ge(s["pv"], o["pv"] + (i + 1) * a.ktiles)
                    act.activation(o_t[:, g, b * S + qc * CH:b * S + (qc + 1) * CH], ps[:, 4, :], ACT.Copy)\
                       .then_inc(s["oev"], 1)

                for n in range(total):
                    if n >= 2:
                        act.wait_ge(s["pv"], o["pv"] + n - 1)
                    for pr in range(2):
                        act.wait_ge(s["sc"], o["sc"] + 2 * n + pr + 1)
                        act.activation(probs[n % 2][0:a.krows, 2 * pr:2 * pr + 2, :],
                                       ps[0:a.krows, 2 * pr:2 * pr + 2, :], ACT.Exp, scale=scale)\
                           .then_inc(s["ex"], 1)
                    if n and n % a.ktiles == 0:
                        copy_sums(n // a.ktiles - 1)
                copy_sums(total // a.ktiles - 1)
                for t in range(NT):
                    act.wait_ge(s["ctp"], o["ctp"] + t + 1)
                    if t >= 2:
                        act.wait_ge(s["yp"], o["yp"] + t - 1)
                    act.activation(ctxn_t[t % 2][:, :, :],
                                   ps[:, 2 + t % 2, 0:D].rearrange("p (k n) -> p k n", k=KD), ACT.Copy)\
                       .then_inc(s["cev"], 1)

            def experts():
                act.wait_ge(m["b2"], 32)
                act.wait_ge(m["ex_in"], 1)
                act.activation(gl[:, :, :], gm[:, :, :], ACT.Exp).then_inc(m["ex"], 1)
                for e in range(E_):
                    for ht in range(F_ // P):
                        u = e * (F_ // P) + ht
                        act.wait_ge(m["h"], u + 1)
                        if e >= 2 and ht == 0:
                            act.wait_ge(m["y"], 2 * (e - 1))
                        act.activation(hid[e % 2][:, ht, :], ps[:, 1 + u % 3, 0:C_], ACT.Relu,
                                       bias=ff_bias[:, u:u + 1]).then_inc(m["hev"], 1)

            def leaves():
                act.wait_ge(f["w"], 16 * 4)
                for u in range(NT // 4):
                    act.wait_ge(f["tp"], u + 1)
                    act.activation(sel_t[0:96, u * CH:(u + 1) * CH], ps[0:96, 4 + u % 2, :], ACT.Copy)\
                       .then_inc(f["selt"], 1)
                hu = yu = 0
                for i in range(3):
                    for c in range(NCH):
                        for ht in range(F_ // P):
                            act.wait_ge(f["h"], hu + 1)
                            if ht == 0 and yu:
                                act.wait_ge(f["y"], yu)
                            act.activation(fh[:, ht, :], ps[:, 5 + hu % 3, :], ACT.Relu, bias=fb1[:, i, ht:ht + 1])\
                               .then_inc(f["hev"], 1)
                            hu += 1
                        yu += 2 if i < 2 else 4
                for t in range(NT):
                    act.wait_ge(f["mx"], t + 1)
                    if t >= 2:
                        act.wait_ge(f["ptp"], t - 1)
                    act.activation(f_p[t % 2], ps[:, 2 * (t % 2):2 * (t % 2) + 2, :].rearrange("p a n -> p (a n)"),
                                   ACT.Exp, bias=f_nmx[:, t:t + 1], scale=D ** -0.5,
                                   accum_out=f_sum[:, t:t + 1]).then_inc(f["ex"], 1)
                    act.wait_ge(f["ptp"], t + 1)
                    if t >= 2:
                        act.wait_ge(f["o"], t - 1)
                    act.activation(f_pt[t % 2][:, 0:4, :], ps[:, 4, :].rearrange("p (k n) -> p k n", n=P), ACT.Copy)\
                       .then_inc(f["ptev"], 1)

            for n in range(SUBLAYERS):
                layer_norm(n)
                if n in AT:
                    a, s, o, _, _ = AT[n]
                    attention(a, s, o)
                elif n == 2:
                    experts()
                else:
                    leaves()

        @block.vector
        def _(dve):
            def stat(n, t):
                return dve.bn_stats(stats[:, t, :], x[:, t, :])

            def layer_norm(n):
                for t in range(NT):
                    last = dve.bn_aggr(mv[:, t, :], stats[:, t, :])
                vlink(dve, last)
                dve.tensor_scalar(ve[:, :], mv[:, :, 1], EPS, None, ALU.add).then_inc(s_ln["ln_var"][n], 1)
                dve.wait_ge(s_ln["ln_sd"][n], 1)
                vlink(dve, dve.reciprocal(rstd[:, :], sd[:, :]))
                vlink(dve, dve.tensor_tensor(tmp_r[:, :], rstd[:, :], rstd[:, :], ALU.mult))
                vlink(dve, dve.tensor_tensor(tmp_r[:, :], tmp_r[:, :], ve[:, :], ALU.mult))
                vlink(dve, dve.tensor_scalar(tmp_r[:, :], tmp_r[:, :], -0.5, 1.5, ALU.mult, ALU.add))
                vlink(dve, dve.tensor_tensor(rstd[:, :], rstd[:, :], tmp_r[:, :], ALU.mult))
                for t in range(NT):
                    dve.tensor_scalar(xn[:, t, :], x[:, t, :], mv[:, t, 0:1], rstd[:, t:t + 1],
                                      ALU.subtract, ALU.mult).then_inc(s_ln["ln_xn"][n], 1)

            def ternary(s, o):
                dve.wait_ge(s_w[0], 16 * 8)
                ws = [weights_of[0][c].rearrange("p k n -> p (k n)") for c in "qkvo"]
                dve.wait_ge(s["tern_tot"], o["tern_tot"] + 1)
                vlink(dve, dve.tensor_scalar(tern_d[:, :], ps[:, 7, 0:4], 1.0 / (D * D), THRESH, ALU.mult, ALU.mult))
                vlink(dve, dve.tensor_scalar(tern_n[:, :], tern_d[:, :], -1.0, None, ALU.mult))
                for i, w in enumerate(ws):
                    dve.scalar_tensor_tensor(w_pos, w_abs[i], tern_d[:, i:i + 1], w_abs[i], ALU.is_gt, ALU.mult,
                                             accum_out=tern_s[:, i:i + 1])
                    vlink(dve, dve.tensor_scalar(w_neg, w_abs[i], tern_d[:, i:i + 1], None, ALU.is_gt))
                    last = dve.tensor_reduce(tern_s[:, 4 + i:5 + i], w_neg, AX.X, ALU.add)
                    if i < 3:
                        vlink(dve, last)
                last.then_inc(s["tern_sum"], 1)
                dve.wait_ge(s["tern_tot"], o["tern_tot"] + 2)
                vlink(dve, dve.tensor_scalar(tern_c[:, :], ps[:, 7, 12:16], 1.0, None, ALU.max))
                vlink(dve, dve.reciprocal(tern_a[:, :], tern_c[:, :]))
                vlink(dve, dve.tensor_tensor(tern_a[:, :], ps[:, 7, 8:12], tern_a[:, :], ALU.mult))
                for i, w in enumerate(ws):
                    dve.tensor_scalar(w_pos, w, tern_d[:, i:i + 1], tern_a[:, i:i + 1], ALU.is_gt, ALU.mult)
                    vlink(dve, dve.tensor_scalar(w_neg, w, tern_n[:, i:i + 1], tern_a[:, i:i + 1],
                                                 ALU.is_lt, ALU.mult))
                    vlink(dve, dve.tensor_tensor(w_pos, w_pos, w_neg, ALU.subtract))
                    vlink(dve, dve.tensor_tensor(w_pos, w_pos, w, ALU.subtract))
                    last = dve.tensor_tensor(w, w, w_pos, ALU.add)
                    if i < 3:
                        vlink(dve, last)
                last.then_inc(s["wready"], 1)

            def attention(a, s, o):
                if a.ternary:
                    ternary(s, o)
                else:
                    dve.wait_ge(s_w[a.index], 16 * weight_loads(a))
                if a.rope:
                    dve.wait_ge(s_rotary, 32)
                wts = weights_of[a.index]
                dve.wait_ge(s_pool0, pool_marks(a))
                done = [0]

                def max_item(n, it):
                    gi = it[1]
                    bank = 5 + n % 3
                    dve.wait_ge(s["mi"], o["mi"] + n + 1)
                    if it[0] == "m":
                        _, _, qt, j, kc = it
                        if a.cross:
                            dst = mx[:, gi % 2, :].rearrange("p (j q) -> p j q", j=4)[:, :, qt]
                            ins = dve.tensor_reduce(dst, ps[:, bank, 0:4 * L].rearrange("p (j n) -> p j n", j=4),
                                                    AX.X, ALU.max)
                        else:
                            ins = dve.tensor_reduce(mx_raw[:, kc, j * 8 + qt:j * 8 + qt + 1], ps[:, bank, :],
                                                    AX.X, ALU.max)
                        ins.then_inc(s["mfree"], 1)
                        if n == a.m_end[gi]:
                            if not a.cross:
                                dve.wait_ge(s["mfree"], o["mfree"] + n + 1)
                                dve.tensor_tensor(mx[:, gi % 2, :], mx_raw[:, 0, :], mx_raw[:, 1, :], ALU.max)\
                                   .then_inc(s["mxr"], 1)
                                dve.wait_ge(s["mxr"], o["mxr"] + gi + 1)
                    else:
                        rp = row_parts[0:32, gi % 2]
                        if gi >= 2:
                            i = (gi - 2) % a.ring
                            dve.wait_ge(s[f"rl{i}"], o[f"rl{i}"] + 48 * ((gi - 2) // a.ring + 1))
                        vlink(dve, dve.tensor_scalar(rp[:, 0, :], ps[0:32, bank, 0:P], -1.0, None, ALU.mult))
                        ins = dve.scalar_tensor_tensor(row_rest[0:32, :], ps[0:32, bank, 0:P], -1.0, rp[:, 0, :],
                                                       ALU.mult, ALU.subtract)
                        ins.then_inc(s["mfree"], 1)
                        dve.wait_ge(s["mfree"], o["mfree"] + n + 1)
                        vlink(dve, dve.tensor_copy(rp[:, 1, :], row_rest[0:32, :]))
                        dve.tensor_tensor(rp[:, 2, :], row_rest[0:32, :], rp[:, 1, :], ALU.subtract)\
                           .then_inc(s["rows"], 1)
                def max_items(limit):
                    for n in range(done[0], min(limit, len(a.items))):
                        max_item(n, a.items[n])
                        done[0] = n + 1

                def turn_halves(u):
                    w, c0 = units(a)[u][4], units(a)[u][3] % S
                    full, r = roped[u % 2][:, 0:w], rest[u % 2][:, 0:w]
                    dve.wait_ge(s["pj_rot"], o["pj_rot"] + u + 1)
                    if u >= 2:
                        dve.wait_ge(s["split"], o["split"] + u - 1)
                    vlink(dve, dve.tensor_tensor(r, ps[:, 2 + u % 2, 0:w], sin_t[:, c0:c0 + w], ALU.mult))
                    dve.wait_ge(s["pj_cos"], o["pj_cos"] + u + 1)
                    dve.tensor_tensor(full, full, r, ALU.add).then_inc(s["pj_roped"], 1)

                def split(u):
                    w, pt = units(a)[u][4], parts[u % PARTS]
                    full, r = (roped if a.rope else proj)[u % 2][:, 0:w], rest[u % 2][:, 0:w]
                    if a.rope:
                        dve.wait_ge(s["pj_roped"], o["pj_roped"] + u + 1)
                    else:
                        dve.wait_ge(s["pj_act"], o["pj_act"] + u + 1)
                    dve.wait_ge(s["hi"], o["hi"] + u + 1)
                    vlink(dve, dve.tensor_tensor(r, full, pt[:, 0, 0:w], ALU.subtract))
                    vlink(dve, dve.tensor_copy(pt[:, 1, 0:w], r))
                    dve.tensor_tensor(pt[:, 2, 0:w], r, pt[:, 1, 0:w], ALU.subtract).then_inc(s["split"], 1)

                nu = len(units(a))
                for u in range(nu):
                    if a.rope:
                        if u == 0:
                            turn_halves(0)
                        if u + 1 < nu:
                            turn_halves(u + 1)
                    split(u)
                    if u >= a.early:
                        max_items(done[0] + a.fill)
                if a.cross:
                    vlink(dve, dve.memset(va[64:P, 0:B, :], 0.0))
                    vlink(dve, dve.memset(va[64:L, 0:B, 0:H * VW].rearrange("p t (h n) -> p t h n", n=VW)[:, :, :, DH:],
                                          1.0))
                for t in range(B if a.cross else NT):
                    dve.wait_ge(s["vpj"], o["vpj"] + t + 1)
                    dst = va[0:a.krows, t, 0:H * VW].rearrange("p (h n) -> p h n", n=VW)[:, :, 0:DH]
                    src = ps[0:a.krows, t % 2, 0:D].rearrange("p (h n) -> p h n", n=DH)
                    if a.bias:
                        ins = dve.tensor_tensor(dst, src, wts["bv"][0:a.krows, :].rearrange("p (h n) -> p h n", n=DH), ALU.add)
                    else:
                        ins = dve.tensor_copy(dst, src)
                    ins.then_inc(s["vev"], 1)
                    max_items(done[0] + a.fill)
                max_items(len(a.items))
                if a.index == 0:
                    dve.wait_ge(m["zeroed"], 16)
                n_st = a.index

                def normalise(t):
                    dve.wait_ge(s["otp"], o["otp"] + t + 1)
                    view = ps[:, t % 2, :].rearrange("p (h n) -> p h n", n=32)
                    if a.mixed:
                        vlink(dve, dve.reciprocal(rec[t % 2][:, :], view[:, :, DH]))
                        rows = ctx_rows[:, 4 * (t // 4):4 * (t // 4) + 4, 4 * DH * (t % 4):4 * DH * (t % 4 + 1)]
                        for i in range(4):
                            ins = dve.tensor_tensor(rows[:, :, i * DH:(i + 1) * DH], view[:, 4 * i:4 * i + 4, 0:DH],
                                                    rec[t % 2][:, 4 * i:4 * i + 4].unsqueeze(2)
                                                    .broadcast_to([P, 4, DH]), ALU.mult)
                        ins.then_inc(s["ocx"], 1)
                        return
                    if t >= 2:
                        dve.wait_ge(s["ctp"], o["ctp"] + t - 1)
                    vlink(dve, dve.reciprocal(rec[t % 2][:, :], view[:, :, DH]))
                    dve.tensor_tensor(ctxn[t % 2].rearrange("p (h n) -> p h n", n=DH), view[:, :, 0:DH],
                                      rec[t % 2][:, :].unsqueeze(2).broadcast_to([P, H, DH]), ALU.mult)\
                       .then_inc(s["ocx"], 1)

                def finish(t):
                    dve.wait_ge(s["yp"], o["yp"] + t + 1)
                    y = ps[:, 6 + t % 2, 0:D]
                    if a.quant:
                        ins = dve.tensor_tensor(y_all[:, t, :], y, wts["bo"], ALU.add)
                        ins.then_inc(s["yev"], 1)
                        dve.wait_ge(s["yev"], o["yev"] + t + 1)
                        ins = dve.tensor_reduce(tmp_r[:, t:t + 1], y_all[:, t, :], AX.X, ALU.max,
                                                apply_absolute_value=True)
                        if t == NT - 1:
                            vlink(dve, ins)
                        return
                    if a.bias:
                        vlink(dve, dve.tensor_tensor(x[:, t, :], x[:, t, :], wts["bo"], ALU.add))
                    dve.tensor_tensor(x[:, t, :], x[:, t, :], y, ALU.add).then_inc(s["yev"], 1)
                    dve.wait_ge(s["yev"], o["yev"] + t + 1)
                    if t < NT - 1:
                        stat(n_st + 1, t)
                    else:
                        vlink(dve, stat(n_st + 1, t))

                if a.mixed:
                    dve.wait_ge(s_xmix, 48)
                lag = 5 if a.mixed else 2
                for t in range(NT + lag):
                    if t < NT:
                        normalise(t)
                    if t >= lag:
                        finish(t - lag)
                if a.quant:
                    quantise(s, o)

            def quantise(s, o):
                dve.tensor_reduce(y_max[:, 0:1], tmp_r[:, :], AX.X, ALU.max).then_inc(s["ymax"], 1)
                dve.wait_ge(s["ygmax"], o["ygmax"] + 1)
                vlink(dve, dve.tensor_scalar(y_max[:, 2:3], y_max[:, 1:2], 1.0 / QMAX, 1e-8, ALU.mult, ALU.max))
                vlink(dve, dve.reciprocal(y_max[:, 3:4], y_max[:, 2:3]))
                for i in range(2):
                    r = slice(i * NT // 2, (i + 1) * NT // 2)
                    y, z, xr = (v[:, r, :].rearrange("p t n -> p (t n)") for v in (y_all, xn, x))
                    vlink(dve, dve.tensor_scalar(z, y, y_max[:, 3:4], ROUND, ALU.mult, ALU.add))
                    vlink(dve, dve.tensor_scalar(z, z, -ROUND, QMAX, ALU.add, ALU.min))
                    vlink(dve, dve.tensor_scalar(z, z, -QMAX, y_max[:, 2:3], ALU.max, ALU.mult))
                    vlink(dve, dve.tensor_tensor(z, z, y, ALU.subtract))
                    vlink(dve, dve.tensor_tensor(z, y, z, ALU.add))
                    vlink(dve, dve.tensor_tensor(xr, xr, z, ALU.add))
                    for t in range(i * NT // 2, (i + 1) * NT // 2):
                        last = stat(1, t)
                vlink(dve, last)

            def experts():
                dve.wait_ge(m["lg"], 1)
                dve.wait_ge(m["w"], 16)
                lg = ps[:, 4, 0:NT * E_].rearrange("p (t e) -> p t e", e=E_)

                def wide(v):
                    return v.unsqueeze(2).broadcast_to([P, NT, E_])

                dve.memset(onehot_pad[:, 0:before], 0.0)
                vlink(dve, dve.tensor_reduce(g_max[:, :], lg, AX.X, ALU.max))
                dve.tensor_tensor(gm[:, :, :], lg, wide(g_max[:, :]), ALU.subtract).then_inc(m["ex_in"], 1)
                dve.wait_ge(m["ex"], 1)
                vlink(dve, dve.tensor_reduce(g_sum[:, :], gl[:, :, :], AX.X, ALU.add))
                vlink(dve, dve.reciprocal(g_rec[:, :], g_sum[:, :]))
                vlink(dve, dve.tensor_tensor(gl[:, :, :], gl[:, :, :], wide(g_rec[:, :]), ALU.mult))
                vlink(dve, dve.tensor_reduce(g_max[:, :], gl[:, :, :], AX.X, ALU.max))
                vlink(dve, dve.tensor_tensor(gt[:, :, :], gl[:, :, :], wide(g_max[:, :]), ALU.is_equal))
                vlink(dve, dve.tensor_tensor(gt[:, :, :], gt[:, :, :], rev8[:, :, :], ALU.mult))
                vlink(dve, dve.tensor_reduce(g_first[:, :], gt[:, :, :], AX.X, ALU.max))
                vlink(dve, dve.tensor_tensor(onehot[:, :, :], rev8[:, :, :], wide(g_first[:, :]), ALU.is_equal))
                dve.tensor_copy(onehot_b[:, :, :], onehot[:, :, :]).then_inc(m["oh"], 1)
                dve.wait_ge(m["cum"], 1)
                cum = ps[:, 5, 0:NT * E_].rearrange("p (t e) -> p t e", e=E_)
                vlink(dve, dve.scalar_tensor_tensor(gt[:, :, :], cum, -1.0, onehot[:, :, :], ALU.add, ALU.mult))
                vlink(dve, dve.tensor_reduce(g_pos[:, :], gt[:, :, :], AX.X, ALU.add))
                vlink(dve, dve.tensor_scalar(g_keep[:, :], g_pos[:, :], float(C_), None, ALU.is_lt))
                dve.tensor_tensor(g_val[:, :], g_max[:, :], g_keep[:, :], ALU.mult)
                vlink(dve, dve.tensor_scalar(g_off[:, :], g_first[:, :], -float(C_), float(E_ * C_), ALU.mult, ALU.add))
                vlink(dve, dve.tensor_tensor(g_slot[:, :], g_off[:, :], g_pos[:, :], ALU.add))
                vlink(dve, dve.tensor_scalar(g_keep[:, :], g_keep[:, :], -float(4 * N), float(4 * N), ALU.mult, ALU.add))
                vlink(dve, dve.tensor_tensor(g_slot[:, :], g_slot[:, :], g_keep[:, :], ALU.add))
                dve.tensor_copy(slot_put[:, :], g_slot[:, :])
                vlink(dve, dve.tensor_scalar(g_pos[:, :], g_pos[:, :], float(C_ - 1), None, ALU.min))
                vlink(dve, dve.tensor_tensor(g_slot[:, :], g_off[:, :], g_pos[:, :], ALU.add))
                dve.tensor_copy(slot_get[:, :], g_slot[:, :]).then_inc(m["slots"], 1)
                dve.wait_ge(m["b2"], 32)

                def take(e):
                    dve.wait_ge(m["tp"], e + 1)
                    if e >= 2:
                        dve.wait_ge(m["h"], (e - 1) * (F_ // P))
                    dve.tensor_copy(disp_t[e % 2][:, :, :], ps[:, 0, :].rearrange("p (k n) -> p k n", k=KD))\
                       .then_inc(m["dt"], 1)

                take(0)
                for e in range(E_):
                    if e + 1 < E_:
                        take(e + 1)
                    for c in range(2):
                        v = 2 * e + c
                        dve.wait_ge(m["y"], v + 1)
                        if e >= 2 and c == 0:
                            dve.wait_ge(m[f"st{e % 2}"], 16 * (e // 2))
                        dve.tensor_tensor(eo[e % 2][:, c, :], ps[:, 6 + v % 2, 0:D], b2_all[:, e, :], ALU.add)\
                           .then_inc(m["yev"], 1)
                for i in range(4):
                    dve.wait_ge(m[f"get{i}"], 16 * 4)
                    for t in range(4 * i, 4 * i + 4):
                        dve.scalar_tensor_tensor(x[:, t, :], back[:, t, :], g_val[:, t:t + 1], x[:, t, :],
                                                 ALU.mult, ALU.add).then_inc(m["xadd"], 1)
                    for t in range(4 * i, 4 * i + 4):
                        dve.wait_ge(m["xadd"], t + 1)
                        last = stat(3, t)
                vlink(dve, last)

            def leaves():
                dve.wait_ge(f["w"], 16 * 4)
                dve.wait_ge(f["nodes"], 32)
                dve.memset(sel[:, :, :], 0.0)
                for i in range(3):
                    dve.wait_ge(f["leafc"], 16 * (i + 1))
                    dve.tensor_copy(leaf_b[i][0:96, :], leaf_f[0:96, :]).then_inc(f["ndev"], 1)
                dve.wait_ge(f["nd"], 1)
                for a in range(2):
                    vlink(dve, dve.tensor_tensor(
                        go[:, 8 * a:8 * a + 8, :], ps[:, 2 + a, 0:384].rearrange("p (t n) -> p t n", n=48),
                        node_b[:, :].unsqueeze(1).broadcast_to([P, 8, 48]), ALU.add))
                vlink(dve, dve.tensor_scalar(go[:, :, :], go[:, :, :], 0.0, None, ALU.is_ge))
                g3 = go.rearrange("p t (i n) -> p (t i) n", n=16)
                vlink(dve, dve.tensor_copy(path[0][:, :, 1:2], g3[:, :, 0:1]))
                vlink(dve, dve.tensor_scalar(path[0][:, :, 0:1], g3[:, :, 0:1], -1.0, 1.0, ALU.mult, ALU.add))
                for lv in range(1, 4):
                    w = 1 << lv
                    par = path[lv - 1][:, :, :]
                    if lv < 3:
                        ch = path[lv].rearrange("p a (n c) -> p a n c", c=2)
                    else:
                        ch = sel.rearrange("p t (i n) -> p (t i) n", n=32)[:, :, 0:16]\
                                .rearrange("p a (n c) -> p a n c", c=2)
                    vlink(dve, dve.tensor_tensor(ch[:, :, :, 1], par, g3[:, :, w - 1:2 * w - 1], ALU.mult))
                    last = dve.tensor_tensor(ch[:, :, :, 0], par, ch[:, :, :, 1], ALU.subtract)
                    if lv < 3:
                        vlink(dve, last)
                last.then_inc(f["sel"], 1)
                for u in range(NT // 4):
                    dve.wait_ge(f["selt"], u + 1)
                    dve.tensor_scalar(nsel_t[0:96, u * CH:(u + 1) * CH], ps[0:96, 4 + u % 2, :], -1.0, 1.0,
                                      ALU.mult, ALU.add).then_inc(f["nselt"], 1)
                yu = 0
                for i in range(3):
                    for c in range(NCH):
                        if i < 2:
                            for k in range(KD):
                                dve.wait_ge(f["y"], yu + 1)
                                dve.tensor_copy((fq_t, fk_t)[i][:, k, c * CH:(c + 1) * CH], ps[:, yu % 2, :])\
                                   .then_inc(f["yev"], 1)
                                yu += 1
                        else:
                            for t in range(4):
                                dve.wait_ge(f["y"], yu + 1)
                                dve.tensor_copy(fv[:, 4 * c + t, :], ps[:, yu % 2, 0:D]).then_inc(f["yev"], 1)
                                yu += 1

                def maxima(t):
                    dve.wait_ge(f["sc"], t + 1)
                    vlink(dve, dve.tensor_reduce(f_mx[:, t:t + 1], ps[:, 2 * (t % 2):2 * (t % 2) + 2, :]
                                                 .rearrange("p a n -> p (a n)"), AX.X, ALU.max))
                    dve.tensor_scalar(f_nmx[:, t:t + 1], f_mx[:, t:t + 1], -(D ** -0.5), None, ALU.mult)\
                       .then_inc(f["mx"], 1)

                dve.wait_ge(s_xback, 16 * B + 16)
                maxima(0)
                for t in range(NT):
                    if t + 1 < NT:
                        maxima(t + 1)
                    dve.wait_ge(f["ptp"], t + 1)
                    if t >= 2:
                        dve.wait_ge(f["o"], t - 1)
                    dve.tensor_copy(f_pt[t % 2][:, 4:8, :], ps[:, 5, :].rearrange("p (k n) -> p k n", n=P))\
                       .then_inc(f["ptev_v"], 1)
                    if t:
                        weigh(t - 1)
                weigh(NT - 1)

            def weigh(t):
                dve.wait_ge(f["o"], t + 1)
                vlink(dve, dve.reciprocal(f_rec[:, t:t + 1], f_sum[:, t:t + 1]))
                dve.scalar_tensor_tensor(x[:, t, :], ps[:, 6 + t % 2, 0:D], f_rec[:, t:t + 1], x[:, t, :],
                                         ALU.mult, ALU.add).then_inc(f["oev"], 1)

            for t in range(NT):
                if t % 4 == 0:
                    dve.wait_ge(s_x[t // 4], 16)
                last = stat(0, t)
            vlink(dve, last)
            for n in range(SUBLAYERS):
                layer_norm(n)
                if n == 0:
                    dve.wait_ge(s_const, 16 * 5)
                    dve.tensor_copy(tri_b[:, :], tri_f[:, :])
                    dve.tensor_copy(ones_b[:, :], ones[:, :]).then_inc(s_castc, 1)
                if n in AT:
                    a, s, o, _, _ = AT[n]
                    attention(a, s, o)
                elif n == 2:
                    experts()
                else:
                    leaves()

        @block.gpsimd
        def _(pool):
            for n in range(SUBLAYERS):
                if n in AT:
                    a, s, o, _, _ = AT[n]
                    if n == 3:
                        pool.wait_ge(m["xadd"], NT)
                    if n in (0, 3):
                        pool.memset(va[:, :, :], 1.0).then_inc(s_pool0, 1)
                        for i in range(3):
                            pool.wait_ge(s_pool0, 4 * (n // 3) + i + 1)
                            pool.memset(k_stack[i][STACK:STACK + 3, :, :], 1.0).then_inc(s_pool0, 1)
                    if n == 0:
                        pool.wait_ge(s_pool0, 4)
                        pool.memset(ctxn[0], 0.0).then_inc(m["zero"], 1)
                    if a.rope:
                        pool.wait_ge(s_rotary, 32)
                        pool.wait_ge(s_pool0, pool_marks(a))
                        for u, (_, _, _, c, w) in enumerate(units(a)):
                            pool.wait_ge(s["pj_act"], o["pj_act"] + u + 1)
                            if u >= 2:
                                pool.wait_ge(s["split"], o["split"] + u - 1)
                            if u:
                                pool.wait_ge(s["pj_cos"], o["pj_cos"] + u)
                            pool.tensor_tensor(roped[u % 2][:, 0:w], proj[u % 2][:, 0:w],
                                               cos_t[:, c % S:c % S + w], ALU.mult).then_inc(s["pj_cos"], 1)
                    for gi in range(B * G):
                        if n == 0 and gi == 2:
                            pool.wait_ge(m["zero"], 1)
                            pool.dma_start(disp_d.rearrange("(p r) n -> p r n", p=P),
                                           ctxn[0].unsqueeze(1).broadcast_to([P, NT, D])).then_inc(m["zeroed"], 16)
                        pool.wait_ge(s["rows"], o["rows"] + gi + 1)
                        for r in range(3):
                            pool.dma_start(q_ring[gi % a.ring][STACK + r:STACK + r + 1, :, :]
                                           .rearrange("p j (q n) -> p (j q) n", n=P),
                                           row_parts[0:32, gi % 2, r, :]).then_inc(s[f"rl{gi % a.ring}"], 16)
                    if a.quant:
                        pool.wait_ge(s["ymax"], o["ymax"] + 1)
                        pool.partition_all_reduce(y_max[:, 1:2], y_max[:, 0:1], P, bass.bass_isa.ReduceOp.max)\
                            .then_inc(s["ygmax"], 1)
                elif n == 2:
                    pool.wait_ge(m["zeroed"], 16)
                    pool.wait_ge(m["slots"], 1)
                    for t in range(NT):
                        pool.indirect_dma_start(
                            disp_d, bass.IndirectOffsetOnAxis(ap=slot_put[:, t:t + 1], axis=0), xn[:, t, :], None,
                            bounds_check=N - 1, oob_is_err=False).then_inc(m["put"], 16)
                    pool.wait_ge(m["st0"], 16 * E_ // 2)
                    pool.wait_ge(m["st1"], 16 * E_ // 2)
                    for t in range(NT):
                        pool.indirect_dma_start(
                            back[:, t, :], None, eo_d, bass.IndirectOffsetOnAxis(ap=slot_get[:, t:t + 1], axis=0),
                            bounds_check=N - 1, oob_is_err=False).then_inc(m[f"get{t // 4}"], 16)

        @block.sync
        def _(sp):
            def attention_weights(a):
                w, to, done_ = d[a.name], weights_of[a.index], s_w[a.index]
                for c in "qkvo":
                    sp.dma_start(to[c][:, :, :], w["w" + c].rearrange("(k p) n -> p k n", p=P)).then_inc(done_, 16)
                if a.bias:
                    sp.dma_start(to["bq"], w["bq"]).then_inc(done_, 16)
                    sp.dma_start(to["bk"], w["bk"]).then_inc(done_, 16)
                    sp.dma_start(to["bv"], w["bv"].unsqueeze(0).broadcast_to([P, D])).then_inc(done_, 16)
                    sp.dma_start(to["bo"], w["bo"].unsqueeze(0).broadcast_to([P, D])).then_inc(done_, 16)
                if a.cross:
                    sp.dma_start(ctx_t[:, :, :], d["ctx_t"].rearrange("(k p) n -> p k n", p=P)).then_inc(done_, 16)

            def expert_weights(e):
                if e >= 3:
                    sp.wait_ge(m["y"], 2 * (e - 2))
                sp.dma_start(w1e[e % 3][:, :, :], d["moe"]["w1"][e].rearrange("(k p) n -> p k n", p=P))\
                  .then_inc(m[f"w1_{e % 3}"], 16)
                sp.dma_start(w2e[e % 3][:, :, :], d["moe"]["w2"][e].rearrange("(k p) n -> p k n", p=P))\
                  .then_inc(m[f"w1_{e % 3}"], 16)

            def tree_weights(i):
                sp.dma_start(fw1[i % 2][:, :, :], d["fff"][f"w1{i}"].rearrange("(k p) n -> p k n", p=P))\
                  .then_inc(f[f"wl{i % 2}"], 16)
                sp.dma_start(fw2[i % 2][:, :, :], d["fff"][f"w2{i}"].rearrange("(k p) n -> p k n", p=P))\
                  .then_inc(f[f"wl{i % 2}"], 16)

            for i in range(4):
                sp.dma_start(x[:, 4 * i:4 * i + 4, :],
                             d["x"].rearrange("(t p) n -> p t n", p=P)[:, 4 * i:4 * i + 4, :]).then_inc(s_x[i], 16)
            for t_, n_ in ((ident, "c_ident"), (rot, "c_rot"), (ones, "c_ones"), (tri_f, "c_tri")):
                sp.dma_start(t_[:, :], d[n_]).then_inc(s_const, 16)
            sp.dma_start(rev8_c[:, :], d["c_rev8"]).then_inc(s_const, 16)
            attention_weights(SELF0)
            attention_weights(CROSS0)
            sp.dma_start(wg[:, :, :], d["moe"]["wg"].rearrange("(k p) n -> p k n", p=P)).then_inc(m["w"], 16)
            sp.dma_start(nodes[:, :, :], d["fff"]["nodes"].rearrange("(k p) n -> p k n", p=P)).then_inc(f["nodes"], 16)
            sp.dma_start(node_b[:, :], d["fff"]["node_b"].unsqueeze(0).broadcast_to([P, 48])).then_inc(f["nodes"], 16)
            expert_weights(0)
            for n in range(SUBLAYERS):
                if n in AT:
                    a, s, o, qp, kp = AT[n]
                    if n:
                        sp.wait_ge(s_ln["ln_xn"][n], 1)
                        scalar_done(sp, n - 1)
                    if n == 1:
                        attention_weights(SELF1)
                    if a.rope:
                        sp.dma_start(cos_t, d["c_cos"]).then_inc(s_rotary, 16)
                        sp.dma_start(sin_t, d["c_sin"]).then_inc(s_rotary, 16)
                    if n == 4:
                        tree_weights(0)
                    if a.mixed:
                        sp.wait_ge(s_ln["ln_xn"][n], NT)
                        sp.dma_start(x_d.rearrange("(t p) n -> p t n", p=P), x[:, :, :]).then_inc(s_xmix, 16)

                    us = units(a)

                    def store(u):
                        which, b, hh, c, w_ = us[u]
                        sp.wait_ge(s["split"], o["split"] + u + 1)
                        dst = (qp if which == "q" else kp)[:, hh * P:(hh + 1) * P, c:c + w_]
                        sp.dma_start(dst.rearrange("s p n -> p s n"), parts[u % PARTS][:, :, 0:w_])\
                          .then_inc(s[f"st{u % PARTS}"], 16)

                    def load(gi, first=0, last=6):
                        b, g = divmod(gi, G)
                        slot = gi % a.ring
                        if first == 0:
                            need = max(u for u in range(len(us)) if us[u][0] == us[-1][0]
                                       and us[u][1:3] == (b, g // 2)) + 1
                            for i in range(PARTS):
                                sp.wait_ge(s[f"st{i}"], o[f"st{i}"] + 16 * len(range(i, need, PARTS)))
                        if a.cross and gi == 0:
                            for blk in range(6):
                                sp.dma_start(keys_all[16 * blk:16 * blk + 16, :, :],
                                             kp[KPART[blk]].rearrange("(h r) n -> r h n", r=DH))\
                                  .then_inc(s["ldk0"], 16)
                        if gi >= a.ring:
                            sp.wait_ge(s["ex"], o["ex"] + 2 * a.steps * (gi - a.ring + 1))
                        for blk in range(first, last):
                            rows = slice(16 * blk, 16 * blk + 16)
                            sp.dma_start(q_ring[slot][rows, :, :],
                                         qp[QPART[blk], 64 * g:64 * g + 64, b * S:(b + 1) * S]
                                         .rearrange("(j r) n -> r j n", r=DH)).then_inc(s[f"ldq{slot}"], 16)
                            if not a.cross:
                                sp.dma_start(k_stack[slot][rows, :, :],
                                             kp[KPART[blk], 64 * g:64 * g + 64, b * S:(b + 1) * S]
                                             .rearrange("(j r) n -> r j n", r=DH)).then_inc(s[f"ldk{slot}"], 16)

                    if a.cross:
                        early = {3: (0, 0, 6), 4: (1, 0, 3), 5: (1, 3, 6), 6: (2, 0, 6), 7: (3, 0, 6), 8: (4, 0, 6)}
                    else:
                        early = {3: (0, 0, 6)}
                        early.update({4 + i: (1, i, i + 1) for i in range(6)})
                        early.update({10 + i: (2, i, i + 1) for i in range(6)})
                    for u in range(len(us)):
                        store(u)
                        if u in early:
                            load(*early[u])
                    if a.mixed:
                        sp.wait_ge(s_xmix, 16)
                        for b in range(B):
                            sp.dma_start(x[64 * b:64 * b + 64, :, :],
                                         x_d[b * S:(b + 1) * S, :].rearrange("(t r) n -> r t n", r=64))\
                              .then_inc(s_xmix, 16)
                    for gi in range(a.ring, B * G):
                        load(gi)
                elif n == 2:
                    sp.wait_ge(s_ln["ln_xn"][n], 1)
                    scalar_done(sp, n - 1)
                    w = d["moe"]
                    sp.dma_start(ff_bias, w["b1"]).then_inc(m["b2"], 16)
                    sp.wait_ge(m["b2"], 16)
                    sp.dma_start(b2_all.rearrange("p e n -> p (e n)"),
                                 w["b2"].rearrange("(a e) n -> a (e n)", a=1).broadcast_to([P, E_ * D]))\
                      .then_inc(m["b2"], 16)

                    def tokens(e):
                        if e >= 2:
                            sp.wait_ge(m["tp"], e - 1)
                        sp.dma_start(disp[e % 2][:, :, :],
                                     disp_d[e * C_:(e + 1) * C_, :].rearrange("(c p) n -> p c n", p=P))\
                          .then_inc(m[f"dl{e % 2}"], 16)

                    for e in range(1, 3):
                        expert_weights(e)
                    sp.wait_ge(m["put"], 16 * NT)
                    tokens(0)
                    tokens(1)
                    attention_weights(CROSS1)
                    for e in range(E_):
                        if e + 2 < E_:
                            tokens(e + 2)
                        sp.wait_ge(m["yev"], 2 * e + 2)
                        sp.dma_start(eo_d[e * C_:(e + 1) * C_, :].rearrange("(c p) n -> p c n", p=P), eo[e % 2][:, :, :])\
                          .then_inc(m[f"st{e % 2}"], 16)
                        if e + 3 < E_:
                            expert_weights(e + 3)
                else:
                    sp.wait_ge(s_ln["ln_xn"][n], 1)
                    scalar_done(sp, n - 1)
                    w = d["fff"]
                    sp.dma_start(fb2[0:96, :, :], w["b2"]).then_inc(f["w"], 16)
                    for i in range(3):
                        sp.dma_start(fb1[:, i, :], w[f"b1{i}"]).then_inc(f["w"], 16)
                    for i in range(3):
                        if i:
                            sp.wait_ge(f["ndev"], i)
                        sp.dma_start(leaf_f[0:96, :], d["c_leaf"][i]).then_inc(f["leafc"], 16)
                    sp.wait_ge(s_ln["ln_xn"][n], NT)
                    for b in range(B):
                        sp.dma_start(x_mixed_d[b * S:(b + 1) * S, :].rearrange("(t r) n -> r t n", r=64),
                                     x[64 * b:64 * b + 64, :, :]).then_inc(s_xback, 16)
                    for i in range(3):
                        if i == 2:
                            sp.wait_ge(s_xback, 16 * B)
                            sp.dma_start(x[:, :, :], x_mixed_d.rearrange("(t p) n -> p t n", p=P))\
                              .then_inc(s_xback, 16)
                            sp.wait_ge(f["y"], 2 * NCH)
                        if i:
                            tree_weights(i)
            for i in range(4):
                sp.wait_ge(f["oev"], 4 * i + 4)
                sp.dma_start(out.rearrange("(t p) n -> p t n", p=P)[:, 4 * i:4 * i + 4, :],
                             x[:, 4 * i:4 * i + 4, :]).then_inc(s_out, 16)
            sp.wait_ge(s_out, 16 * 4)


def _constants():
    import numpy as np

    c = {"c_ident": np.eye(P, dtype=np.float32), "c_ones": np.ones((P, P), np.float32)}
    c["c_tri"] = np.triu(np.ones((P, P), np.float32))
    c["c_rev8"] = np.tile((E_ - np.arange(E_)).astype(np.float32), (P, NT))
    rot = np.zeros((P, P), np.float32)
    for h in range(P // DH):
        for i in range(DH // 2):
            rot[h * DH + 2 * i + 1, h * DH + i] = -1.0
            rot[h * DH + 2 * i, h * DH + DH // 2 + i] = 1.0
    c["c_rot"] = rot
    inv = np.float32(1.0) / np.power(np.float32(10000.0), np.arange(0, DH, 2, dtype=np.float32) / np.float32(DH))
    fr = np.arange(S, dtype=np.float32)[:, None] * inv[None, :]
    emb = np.concatenate([fr, fr], axis=-1)
    c["c_cos"] = np.ascontiguousarray(np.tile(np.cos(emb).astype(np.float32).T, (P // DH, 1)))
    c["c_sin"] = np.ascontiguousarray(np.tile(np.sin(emb).astype(np.float32).T, (P // DH, 1)))
    leaf = np.zeros((3, 96, F_), np.float32)
    for i in range(3):
        for n in range(NLEAF):
            leaf[i, 32 * i + n, n * LEAFW:(n + 1) * LEAFW] = NEG
    c["c_leaf"] = leaf
    return c


def kernel(**inputs):
    import numpy as np
    import concourse.bacc as bacc
    from concourse.bass_utils import run_bass_kernel_spmd as run

    a = {k: np.asarray(v) for k, v in inputs.items()}
    arrays = dict(_constants())
    arrays["x"] = a["x"].reshape(N, D)
    arrays["ctx_t"] = a["ctx_1024"].reshape(B * L, D).T
    names = {"self0": ("L0_attn_W", "L0_attn_b", "qkvo"), "cross0": ("L0_xattn_w", "L0_xattn_b", "qkvo"),
             "self1": ("L1_attn_W", None, "qkvo"), "cross1": ("L1_xattn_W", "L1_xattn_b", "qkvh")}
    for st, (w, b, cs) in names.items():
        for c, to in zip(cs, "qkvo"):
            arrays[f"{st}.w{to}"] = a[w + c].T
            if b:
                arrays[f"{st}.b{to}"] = a[b + c].reshape(KD, P).T if to in "qk" else a[b + c]
    for n in ("wg", "w1", "b1", "w2", "b2"):
        arrays["moe." + n] = a["L0_ffn_" + n]
    arrays["moe.b1"] = arrays["moe.b1"].reshape(E_ * F_ // P, P).T
    nodes, node_b = np.zeros((D, 48), np.float32), np.zeros(48, np.float32)
    b2 = np.zeros((96, 3, D), np.float32)
    for i, c in enumerate("qkv"):
        p = f"L1_ffn_{c}_"
        nodes[:, 16 * i:16 * i + NNODE] = a[p + "node_w"].T
        node_b[16 * i:16 * i + NNODE] = a[p + "node_b"]
        b2[32 * i:32 * i + NLEAF, i, :] = a[p + "b2"]
        arrays[f"fff.w1{i}"] = a[p + "w1"].transpose(1, 0, 2).reshape(D, F_)
        arrays[f"fff.w2{i}"] = a[p + "w2"].reshape(F_, D)
        arrays[f"fff.b1{i}"] = a[p + "b1"].reshape(F_ // P, P).T
    arrays["fff.nodes"], arrays["fff.node_b"], arrays["fff.b2"] = nodes, node_b, b2
    arrays = {k: np.ascontiguousarray(v) for k, v in arrays.items()}

    nc = bacc.Bacc("TRN2", target_bir_lowering=False, num_devices=1)
    d, feed = {}, {}
    for k, v in arrays.items():
        name = "in_" + k.replace(".", "_")
        feed[name] = v
        ap = nc.dram_tensor(name, v.shape, mybir.dt.from_np(v.dtype), kind="ExternalInput").ap()
        if "." in k:
            st, w = k.split(".")
            d.setdefault(st, {})[w] = ap
        else:
            d[k] = ap
    out = nc.dram_tensor("out", (N, D), F32, kind="ExternalOutput").ap()
    decoder_kernel(nc, d, out)
    r = run(nc, [feed], core_ids=[0])
    return r.results[0]["out"].reshape(B, S, D)
```
